# Optimizing a Trainium2 kernel written in Bass

```python
import numpy as np
import jax
import jax.numpy as jnp

def _softmax(x, axis=-1):
    return jax.nn.softmax(x, axis=axis)

def _gelu(x):
    return jax.nn.gelu(x, approximate=True)

def _silu(x):
    return jax.nn.silu(x)

def _sigmoid(x):
    return jax.nn.sigmoid(x)

def _layernorm(x, axis=-1, eps=1e-05):
    m = jnp.mean(x, axis=axis, keepdims=True)
    v = jnp.var(x, axis=axis, keepdims=True)
    return (x - m) / jnp.sqrt(v + eps)

def _scatter_add(tgt, idx, src, axis=0):
    return tgt.at[idx].add(src)

def _segment_sum(src, seg, n):
    return jax.ops.segment_sum(src, seg, n)
kernel_name = 'mk_sandwich_d1_jaxref_r4_a0256f'

def setup_inputs(seed: int=0):
    np.random.seed(seed)
    _w = jnp.asarray

    def _L0_attn_setup():
        import jax, jax.numpy as jnp
        import numpy as np
        B, T, HID = (16, 128, 256)
        NH, NKV, D = (8, 4, 128)
        THETA = 10000.0

        def _rotate_half(x):
            x1, x2 = (x[..., :x.shape[-1] // 2], x[..., x.shape[-1] // 2:])
            return jnp.concatenate((-x2, x1), axis=-1)
        key = jax.random.key(seed)
        k0, k1, k2, k3, k4 = jax.random.split(key, 5)
        s = 0.02
        return {'hidden_states': jax.random.normal(k0, (B, T, HID), dtype=jnp.float32), 'Wq': s * jax.random.normal(k1, (HID, NH * D), dtype=jnp.float32), 'Wk': s * jax.random.normal(k2, (HID, NKV * D), dtype=jnp.float32), 'Wv': s * jax.random.normal(k3, (HID, NKV * D), dtype=jnp.float32), 'Wo': s * jax.random.normal(k4, (NH * D, HID), dtype=jnp.float32)}
    _L0_attn_in = _L0_attn_setup()

    def _L0_ffn_setup():
        import jax, jax.numpy as jnp
        import numpy as np
        N_EXPERTS = 8
        TOP_K = 2
        D_MODEL = 256
        HIDDEN = 1024
        ROUTED_H = 256
        BATCH, SEQ = (2, 1024)
        key = jax.random.key(seed)
        ks = jax.random.split(key, 8)
        std = 0.02
        return {'x': jax.random.normal(ks[0], (BATCH, SEQ, D_MODEL), dtype=jnp.float32), 'w12': std * jax.random.normal(ks[1], (N_EXPERTS, 2 * ROUTED_H, D_MODEL), dtype=jnp.float32), 'w3': std * jax.random.normal(ks[2], (N_EXPERTS, D_MODEL, ROUTED_H), dtype=jnp.float32), 'shared_w1': std * jax.random.normal(ks[3], (HIDDEN, D_MODEL), dtype=jnp.float32), 'shared_w2': std * jax.random.normal(ks[4], (HIDDEN, D_MODEL), dtype=jnp.float32), 'shared_w3': std * jax.random.normal(ks[5], (D_MODEL, HIDDEN), dtype=jnp.float32), 'router_w': std * jax.random.normal(ks[6], (N_EXPERTS, D_MODEL), dtype=jnp.float32), 'expert_bias': jnp.zeros((N_EXPERTS,), dtype=jnp.float32)}
    _L0_ffn_in = _L0_ffn_setup()
    _d = {'L0_attn_hidden_states': _L0_attn_in['hidden_states'], 'L0_attn_Wq': _L0_attn_in['Wq'], 'L0_attn_Wk': _L0_attn_in['Wk'], 'L0_attn_Wv': _L0_attn_in['Wv'], 'L0_attn_Wo': _L0_attn_in['Wo'], 'L0_ffn_w12': _L0_ffn_in['w12'], 'L0_ffn_w3': _L0_ffn_in['w3'], 'L0_ffn_shared_w1': _L0_ffn_in['shared_w1'], 'L0_ffn_shared_w2': _L0_ffn_in['shared_w2'], 'L0_ffn_shared_w3': _L0_ffn_in['shared_w3'], 'L0_ffn_router_w': _L0_ffn_in['router_w'], 'L0_ffn_expert_bias': _L0_ffn_in['expert_bias']}
    _x0 = _d['L0_attn_hidden_states']
    _d['L0_attn_hidden_states'] = jax.random.normal(jax.random.fold_in(jax.random.key(seed), 1), (16, 512, 256), dtype=_x0.dtype)
    del _x0
    return _d

def reference(L0_attn_hidden_states, L0_attn_Wq, L0_attn_Wk, L0_attn_Wv, L0_attn_Wo, L0_ffn_w12, L0_ffn_w3, L0_ffn_shared_w1, L0_ffn_shared_w2, L0_ffn_shared_w3, L0_ffn_router_w, L0_ffn_expert_bias):

    def _L0_attn_ref(hidden_states, Wq, Wk, Wv, Wo):
        import jax, jax.numpy as jnp
        import numpy as np
        B, T, HID = (16, 128, 256)
        NH, NKV, D = (8, 4, 128)
        THETA = 10000.0

        def _rotate_half(x):
            x1, x2 = (x[..., :x.shape[-1] // 2], x[..., x.shape[-1] // 2:])
            return jnp.concatenate((-x2, x1), axis=-1)
        b, t, _ = hidden_states.shape
        q = (hidden_states @ Wq).reshape(b, t, NH, D).transpose(0, 2, 1, 3)
        k = (hidden_states @ Wk).reshape(b, t, NKV, D).transpose(0, 2, 1, 3)
        v = (hidden_states @ Wv).reshape(b, t, NKV, D).transpose(0, 2, 1, 3)
        inv_freq = 1.0 / THETA ** (jnp.arange(0, D, 2, dtype=jnp.float32) / D)
        freqs = jnp.outer(jnp.arange(t, dtype=jnp.float32), inv_freq)
        emb = jnp.concatenate((freqs, freqs), axis=-1)
        cos, sin = (jnp.cos(emb), jnp.sin(emb))
        q = q * cos + _rotate_half(q) * sin
        k = k * cos + _rotate_half(k) * sin
        groups = NH // NKV
        k = jnp.repeat(k, groups, axis=1)
        v = jnp.repeat(v, groups, axis=1)
        scale = 1.0 / jnp.sqrt(jnp.float32(D))
        attn = jnp.einsum('bhtd,bhsd->bhts', q, k) * scale
        causal = jnp.triu(jnp.ones((t, t), dtype=bool), k=1)
        attn = jnp.where(causal, -jnp.inf, attn)
        attn = jax.nn.softmax(attn, axis=-1)
        out = jnp.einsum('bhts,bhsd->bhtd', attn, v)
        out = out.transpose(0, 2, 1, 3).reshape(b, t, NH * D)
        return out @ Wo

    def _L0_ffn_ref(x, w12, w3, shared_w1, shared_w2, shared_w3, router_w, expert_bias):
        import jax, jax.numpy as jnp
        import numpy as np
        N_EXPERTS = 8
        TOP_K = 2
        D_MODEL = 256
        HIDDEN = 1024
        ROUTED_H = 256
        BATCH, SEQ = (2, 1024)
        b, s, d = x.shape
        xf = x.reshape(-1, d)
        shared = jax.nn.silu(xf @ shared_w1.T) * (xf @ shared_w2.T) @ shared_w3.T
        scores = jax.nn.sigmoid(xf @ router_w.T)
        _, top_idx = jax.lax.top_k(scores + expert_bias, TOP_K)
        mask = jax.nn.one_hot(top_idx, N_EXPERTS, dtype=xf.dtype).sum(axis=-2)
        gates = scores * mask
        h12 = jnp.einsum('td,ehd->teh', xf, w12)
        h1, h2 = jnp.split(h12, 2, axis=-1)
        h = jax.nn.silu(h1) * h2 * gates[:, :, None]
        routed = jnp.einsum('teh,edh->td', h, w3)
        return (shared + routed).reshape(b, s, d)
    x = L0_attn_hidden_states
    x = x + _layernorm(_L0_attn_ref(_layernorm(x, axis=-1), L0_attn_Wq, L0_attn_Wk, L0_attn_Wv, L0_attn_Wo), axis=-1)
    x = x + _layernorm(_L0_ffn_ref(_layernorm(x, axis=-1), L0_ffn_w12, L0_ffn_w3, L0_ffn_shared_w1, L0_ffn_shared_w2, L0_ffn_shared_w3, L0_ffn_router_w, L0_ffn_expert_bias), axis=-1)
    return x

_drawn_inputs = setup_inputs


def setup_inputs(seed=0):
    import zlib

    import numpy as np

    out = dict(_drawn_inputs(seed))
    spreads = {'L0_ffn_expert_bias': (0.0, 0.1)}
    factors = {}
    for name, (base, spread) in spreads.items():
        noise = np.random.default_rng([zlib.crc32(name.encode()), seed]).standard_normal(out[name].shape)
        drawn = base * np.exp(spread * noise) if base else spread * noise
        out[name] = jnp.asarray(drawn.astype(out[name].dtype))
    for name, factor in factors.items():
        out[name] = (out[name] * factor).astype(out[name].dtype)
    return out
```

```python
from contextlib import ExitStack

import numpy as np

import concourse.bass as bass
from concourse import mybir

F32 = mybir.dt.float32
F32R = mybir.dt.float32r
BF16 = mybir.dt.bfloat16
ALU = mybir.AluOpType
ACT = mybir.ActivationFunctionType
AX_X = mybir.AxisListType.X

P = 128
B, T, C = 16, 512, 256
NH, NKV, D = 8, 4, 128
KC = C // P
NT = T // P
NP = NH // 2
NE = 8
TOP_K = 2
HID = 1024
HE = 256
KH = HE // P
BLOCKS = B
TOKEN_TILES = B * NT
TILES = TOP_K * TOKEN_TILES + NE
EPS = 1e-5
THETA = 10000.0
MASKED = -3.0e38
TAKEN = -1.0e30

HI, LO = 0, 1
PASSES = ((HI, HI), (HI, LO), (LO, HI))

UNITS = (
    ((0, 3, 0),),
    ((1, 3, 0),),
    ((0, 2, 0), (0, 0, 384)),
    ((1, 2, 0), (1, 0, 384)),
    ((0, 1, 0), (1, 1, 256)),
)
NU = len(UNITS)

RING_START = 5
RING_PER_BATCH = 22
RING_ROPE = (0, 7, 10, 15)
RING_V = 3
RING_XT = 13
RING_ROUTER = 18
RING_ROUTER_LAST = 13
RING_ROUTER_END = 17


def wait_if_any(engine, semaphore, count):
    if not isinstance(count, int) or count > 0:
        engine.wait_ge(semaphore, count)


def rows_of(rows, b):
    return rows[b] if isinstance(b, int) else rows[bass.ds(b, 1)].rearrange("b p i c -> (b p) i c")


def attention_phase(nc, x, wq, wk, wv, wo, router_wT, rope_tables, masks, x1, xn2, xs, logits):
    with ExitStack() as ctx:
        def sb(name, shape, dt=F32):
            return ctx.enter_context(nc.sbuf_tensor(name, shape, dt))

        def ps(name):
            return ctx.enter_context(nc.psum_tensor(name, [P, T], F32))

        def sem(name):
            return ctx.enter_context(nc.semaphore(name))

        wq_s = sb("wq_split", [P, 2, KC, NH * D], F32R)
        wk_s = sb("wk_split", [P, 2, KC, NKV * D], F32R)
        wv_s = sb("wv_split", [P, 2, KC, NKV * D], F32R)
        wo_s = sb("wo_split", [P, 2, NH, C], F32R)
        wq_in = sb("wq_in", [P, KC, NH * D])
        wkv_in = sb("wkv_in", [P, 2, KC, NKV * D])
        tables = sb("tables", [P, 4, T])
        mask_in = sb("mask_in", [P, 2, P])
        ident_bf = sb("ident_bf", [P, P], BF16)
        causal_bf = sb("causal_bf", [P, P], BF16)
        eps_t = sb("eps_t", [P, NT])
        mhalf_t = sb("mhalf_t", [P, NT])
        ident = mask_in[:, 0, :]

        x_in = sb("x_in", [P, NT, C])
        x_res = sb("x_res", [P, NT, C])
        xn = sb("xn", [P, NT, C])
        yn = sb("yn", [P, NT, C])
        xn2_sb = wkv_in[:, 0].rearrange("p k n -> p (k n)").rearrange("p (i c) -> p i c", c=C)
        xn2T = wq_in[:, :, 0:T]
        router_w = sb("router_w", [P, KC, NE])
        filler = sb("filler", [P, C])
        x2_stats = sb("x2_stats", [P, NT, 6])
        x2_mv = sb("x2_mv", [P, NT, 2])
        x2_rstd = sb("x2_rstd", [P, NT])
        x2_vare = sb("x2_vare", [P, NT])
        xnT = sb("xnT", [P, 2, KC, T], F32R)
        stats = sb("stats", [P, NT, 6])
        mv = sb("mv", [P, NT, 2])
        rstd = sb("rstd", [P, NT])
        vare = sb("vare", [P, NT])
        y_stats = sb("y_stats", [P, NT, 6])
        y_mv = sb("y_mv", [P, NT, 2])
        y_rstd = sb("y_rstd", [P, NT])
        y_vare = sb("y_vare", [P, NT])

        rope_c = sb("rope_c", [P, 2, T])
        rope_s = sb("rope_s", [P, 2, T])
        roped = sb("roped", [P, 2, T])
        kq = sb("kq", [P, 2, 3, 2, T], F32R)
        v_s = sb("v_split", [P, 2, NT, NKV * D], F32R)
        probs = sb("probs", [P, NU, T])
        wo_in = probs[:, 0:NH * C // T, :].rearrange("p u (h c) -> p (u h) c", c=C)
        neg_max = sb("neg_max", [P, NU, 2])
        row_sum = sb("row_sum", [P, NU, 2])
        row_inv = sb("row_inv", [P, NU, 2])
        pT = sb("pT", [P, 2, 2, NT, T], F32R)
        oT = sb("oT", [P, 2, 2, T], F32R)

        ring = [ps("ring0"), ps("ring1")]
        s_ps = [ps("s_ps0"), ps("s_ps1")]
        t_ps = ps("t_ps")
        o_ps = ps("o_ps")
        y_ps = [ps("y_ps0"), ps("y_ps1")]

        w_loaded = [sem(f"w_loaded{n}") for n in range(4)]
        consts_loaded = sem("consts_loaded")
        x_loaded = sem("x_loaded")
        res_loaded = sem("res_loaded")
        x1_stored = sem("x1_stored")
        w_hi = sem("w_hi")
        w_lo = sem("w_lo")
        masks_ready = sem("masks_ready")
        pool_consts = sem("pool_consts")
        ln_stats = sem("ln_stats")
        ln_mv = sem("ln_mv")
        ln_vare = sem("ln_vare")
        ln_rstd = sem("ln_rstd")
        xn_ready = sem("xn_ready")
        y_st = sem("y_st")
        y_mvs = sem("y_mvs")
        y_ve = sem("y_ve")
        y_rs = sem("y_rs")
        yn_ready = sem("yn_ready")
        x1_ready = sem("x1_ready")
        filler_ready = sem("filler_ready")
        xs_filled = sem("xs_filled")
        xn2_stored = sem("xn2_stored")
        x2_st = sem("x2_st")
        x2_mvs = sem("x2_mvs")
        x2_ve = sem("x2_ve")
        x2_rs = sem("x2_rs")
        xn2_ready = sem("xn2_ready")
        ring_full = sem("ring_full")
        ring_free = sem("ring_free")
        xT_hi = sem("xT_hi")
        v_hi = sem("v_hi")
        rope_sum = sem("rope_sum")
        kq_hi = sem("kq_hi")
        kq_lo = sem("kq_lo")
        scores_ready = sem("scores_ready")
        max_ready = sem("max_ready")
        exp_ready = sem("exp_ready")
        inv_ready = sem("inv_ready")
        probs_ready = sem("probs_ready")
        pT_full = sem("pT_full")
        pT_hi = sem("pT_hi")
        pT_lo = sem("pT_lo")
        o_full = sem("o_full")
        oT_hi = sem("oT_hi")
        oT_lo = sem("oT_lo")
        y_full = sem("y_full")

        x_rows = x.rearrange("b (i p) c -> b p i c", p=P)
        x1_rows = x1.rearrange("b (i p) c -> b p i c", p=P)
        xn2_rows = xn2.rearrange("b (i p) c -> b p i c", p=P)

        def batches(engine, slot_work):
            slot_work(0, True, False)
            with engine.Fori(1, B - 1) as b:
                slot_work(b, False, False)
            slot_work(B - 1, False, True)

        def ring_base(b):
            router_units = RING_PER_BATCH - RING_ROUTER
            return RING_START if isinstance(b, int) and b == 0 else b * RING_PER_BATCH + RING_START - router_units

        def ring_unit(b, offset):
            return ring_base(b) + offset, ring[(RING_START + offset) % 2]

        block = ctx.enter_context(nc.Block())

        @block.sync
        def _(sp):
            sp.dma_start(x_in[:], x_rows[0]).then_inc(x_loaded, 16)
            sp.dma_start(mask_in[:], masks[0:2].rearrange("m p c -> p m c")).then_inc(consts_loaded, 16)
            sp.dma_start(wkv_in[:, 0], wk.rearrange("(k p) n -> p k n", p=P)).then_inc(w_loaded[0], 16)
            sp.dma_start(wq_in[:], wq.rearrange("(k p) n -> p k n", p=P)).then_inc(w_loaded[1], 16)
            sp.dma_start(tables[:], rope_tables.rearrange("m p t -> p m t")).then_inc(consts_loaded, 16)
            sp.dma_start(wkv_in[:, 1], wv.rearrange("(k p) n -> p k n", p=P)).then_inc(w_loaded[2], 16)
            sp.dma_start(wo_in[:], wo.rearrange("(h p) n -> p h n", p=P)).then_inc(w_loaded[3], 16)
            sp.dma_start(router_w[:], router_wT.rearrange("(k p) e -> p k e", p=P)).then_inc(consts_loaded, 16)
            sp.wait_ge(filler_ready, 1)
            for n in range(TILES):
                sp.dma_start(xs[n * P:(n + 1) * P, :], filler[:]).then_inc(xs_filled, 16)

            def work(b, first, last):
                if not last:
                    sp.wait_ge(xn_ready, b + 1)
                    sp.dma_start(x_in[:], rows_of(x_rows, b + 1)).then_inc(x_loaded, 16)
                if not first:
                    sp.wait_ge(x1_ready, b)
                    sp.dma_start(rows_of(x1_rows, b - 1), yn[:]).then_inc(x1_stored, 16)
                sp.dma_start(x_res[:], rows_of(x_rows, b)).then_inc(res_loaded, 16)
                if not first:
                    sp.wait_ge(xn2_ready, b)
                    sp.dma_start(rows_of(xn2_rows, b - 1), xn2_sb).then_inc(xn2_stored, 16)

            batches(sp, work)
            sp.wait_ge(x1_ready, B)
            sp.dma_start(x1_rows[B - 1], yn[:]).then_inc(x1_stored, 16)
            sp.wait_ge(xn2_ready, B)
            sp.dma_start(xn2_rows[B - 1], xn2_sb).then_inc(xn2_stored, 16)
            sp.wait_ge(x1_stored, 16 * B)
            sp.wait_ge(xn2_stored, 16 * B)
            sp.wait_ge(xs_filled, 16 * TILES)

        @block.tensor
        def _(pe):
            def transpose_xn(b_next, unit0, bank_of):
                pe.wait_ge(xn_ready, b_next + 1)
                for k in range(KC):
                    wait_if_any(pe, ring_free, unit0 + k - 1)
                    for i in range(NT):
                        mm = pe.transpose(bank_of(k)[:, i * P:(i + 1) * P], xn[:, i, k * P:(k + 1) * P], ident)
                    mm.then_inc(ring_full, 1)

            def project_pair(j, p, unit, bank):
                wait_if_any(pe, ring_free, unit - 1)
                w, head = (wk_s, p) if j == 0 else (wq_s, 2 * p + j - 1)
                n = 0
                for a, c in PASSES:
                    for k in range(KC):
                        mm = pe.matmul(bank[:], w[:, a, k, head * D:(head + 1) * D], xnT[:, c, k, :],
                                       start=(n == 0), stop=(n == 3 * KC - 1))
                        n += 1
                mm.then_inc(ring_full, 1)

            def project_v(i, unit, bank):
                pe.wait_ge(ring_free, unit - 1)
                n = 0
                for a, c in PASSES:
                    for k in range(KC):
                        mm = pe.matmul(bank[:], xnT[:, a, k, i * P:(i + 1) * P], wv_s[:, c, k, :],
                                       start=(n == 0), stop=(n == 3 * KC - 1))
                        n += 1
                mm.then_inc(ring_full, 1)

            def scores(b, p, u):
                g = b * (NP * NU) + p * NU + u
                pair = b * NP + p
                pe.wait_ge(kq_lo, pair * 3 + (3 if any(h for h, _, _ in UNITS[u]) else 2))
                wait_if_any(pe, exp_ready, g - 1)
                bank = s_ps[(p * NU + u) % 2]
                for h, i, c0 in UNITS[u]:
                    keys = (i + 1) * P
                    for n, (a, c) in enumerate(PASSES):
                        pe.matmul(bank[:, c0:c0 + keys], kq[:, p % 2, 1 + h, a, i * P:(i + 1) * P],
                                  kq[:, p % 2, 0, c, 0:keys], start=(n == 0), stop=False)
                    mm = pe.matmul(bank[:, c0 + i * P:c0 + keys], ident_bf[:], causal_bf[:], start=False, stop=True)
                mm.then_inc(scores_ready, 1)

            def transposes(b, p, u):
                g = b * (NP * NU) + p * NU + u
                pe.wait_ge(probs_ready, g + 1)
                wait_if_any(pe, pT_lo, g)
                for h, i, c0 in UNITS[u]:
                    for j in range(i + 1):
                        c = c0 + j * P
                        mm = pe.transpose(t_ps[:, c:c + P], probs[:, u, c:c + P], ident)
                mm.then_inc(pT_full, 1)

            def values(b, p, h):
                n = b * NH + 2 * p + h
                pair = b * NP + p
                pe.wait_ge(pT_lo, (pair + 1) * NU)
                if p == 0:
                    pe.wait_ge(ring_free, ring_base(b) + RING_V + NT)
                wait_if_any(pe, oT_lo, n)
                for j in range(NT):
                    for m, (a, c) in enumerate(PASSES):
                        mm = pe.matmul(o_ps[:, j * P:T], v_s[:, a, j, p * D:(p + 1) * D], pT[:, c, h, j, j * P:T],
                                       start=(j == 0 and m == 0), stop=(j == NT - 1 and m == 2))
                mm.then_inc(o_full, 1)

            def out_projection(b, p, h):
                n = b * NH + 2 * p + h
                pe.wait_ge(oT_lo, n + 1)
                if p == 0 and h == 0:
                    wait_if_any(pe, yn_ready, b)
                for i in range(NT):
                    for m, (a, c) in enumerate(PASSES):
                        mm = pe.matmul(y_ps[i // 2][:, (i % 2) * C:(i % 2 + 1) * C],
                                       oT[:, a, h, i * P:(i + 1) * P], wo_s[:, c, 2 * p + h, :],
                                       start=(p == 0 and h == 0 and m == 0 and i % 2 == 0),
                                       stop=(p == NP - 1 and h == 1 and m == 2), skip_group_check=True)
                mm.then_inc(y_full, 1)

            def transpose_xn2(b, unit0, bank0):
                pe.wait_ge(xn2_ready, b + 1)
                for k in range(KC):
                    pe.wait_ge(ring_free, unit0 + k - 1)
                    for i in range(NT):
                        mm = pe.transpose(ring[(bank0 + k) % 2][:, i * P:(i + 1) * P], xn2_sb[:, i, k * P:(k + 1) * P],
                                          ident)
                    mm.then_inc(ring_full, 1)

            def route(unit0, bank0):
                for n in range(2):
                    pe.wait_ge(ring_free, unit0 + 2)
                    for i in range(2 * n, 2 * n + 2):
                        for k in range(KC):
                            mm = pe.matmul(ring[(bank0 + n) % 2][:, (i % 2) * NE:(i % 2 + 1) * NE],
                                           xn2T[:, k, i * P:(i + 1) * P], router_w[:, k, :],
                                           start=(k == 0), stop=(k == KC - 1))
                    mm.then_inc(ring_full, 1)

            def work(b, first, last):
                router = RING_ROUTER_LAST if last else RING_ROUTER
                for p in range(NP):
                    more = not (last and p == NP - 1)
                    before = not (first and p == 0)
                    pb, pp = (b, p - 1) if p else (b - 1, NP - 1)

                    def project(j):
                        if more:
                            if j == 0 and p == NP - 1:
                                pe.wait_ge(ring_free, ring_base(b) + RING_XT + KC)
                            project_pair(j, (p + 1) % NP, *ring_unit(b, RING_ROPE[p] + j))

                    def project_values(i):
                        if p == 0:
                            project_v(i, *ring_unit(b, RING_V + i))

                    scores(b, p, 0)
                    if before:
                        transposes(pb, pp, 3)
                    project(0)

                    scores(b, p, 1)
                    if before:
                        transposes(pb, pp, 4)
                    project(1)
                    if before:
                        values(pb, pp, 0)

                    scores(b, p, 2)
                    if before:
                        values(pb, pp, 1)
                    transposes(b, p, 0)

                    scores(b, p, 3)
                    transposes(b, p, 1)
                    project(2)
                    project_values(0)
                    if p == 3 and not first:
                        transpose_xn2(b - 1, ring_base(b) + router, RING_START + router)
                    if before:
                        out_projection(pb, pp, 0)
                    project_values(1)

                    scores(b, p, 4)
                    transposes(b, p, 2)
                    project_values(2)
                    if p == 2 and not last:
                        transpose_xn(b + 1, ring_unit(b, RING_XT)[0], lambda k: ring_unit(0, RING_XT + k)[1])
                    if before:
                        out_projection(pb, pp, 1)
                    project_values(3)
                    if p == 3 and not first:
                        route(ring_base(b) + router, RING_START + router)

            pe.wait_ge(consts_loaded, 48)
            transpose_xn(0, 0, lambda k: ring[k % 2])
            pe.wait_ge(masks_ready, 2)
            pe.wait_ge(w_lo, 2)
            pe.wait_ge(ring_free, KC)
            for j in range(3):
                project_pair(j, 0, KC + j, ring[(KC + j) % 2])
            pe.wait_ge(w_lo, 4)
            batches(pe, work)
            for u in (3, 4):
                transposes(B - 1, NP - 1, u)
            for h in range(2):
                values(B - 1, NP - 1, h)
            for h in range(2):
                out_projection(B - 1, NP - 1, h)
            end = ring_base(B - 1) + RING_ROUTER_END
            transpose_xn2(B - 1, end, RING_START + RING_ROUTER_END)
            route(end, RING_START + RING_ROUTER_END)

        @block.scalar
        def _(act):
            def high_part(out, in_):
                return act.activation(out, in_, ACT.Copy)

            def exponentials(b, p, u):
                g = b * (NP * NU) + p * NU + u
                act.wait_ge(max_ready, g + 1)
                for n, (h, i, c0) in enumerate(UNITS[u]):
                    keys = (i + 1) * P
                    ex = act.activation(probs[:, u, c0:c0 + keys], s_ps[(p * NU + u) % 2][:, c0:c0 + keys], ACT.Exp,
                                        bias=neg_max[:, u, n:n + 1], accum_out=row_sum[:, u, n:n + 1])
                ex.then_inc(exp_ready, 1)

            def normalise(b, p, u):
                g = b * (NP * NU) + p * NU + u
                act.wait_ge(inv_ready, g + 1)
                for n, (h, i, c0) in enumerate(UNITS[u]):
                    keys = (i + 1) * P
                    nm = act.activation(probs[:, u, c0:c0 + keys], probs[:, u, c0:c0 + keys], ACT.Copy,
                                        scale=row_inv[:, u, n:n + 1])
                nm.then_inc(probs_ready, 1)

            def pT_high(b, p, u):
                g = b * (NP * NU) + p * NU + u
                act.wait_ge(pT_full, g + 1)
                if u == 0:
                    wait_if_any(act, o_full, (b * NP + p) * 2)
                for h, i, c0 in UNITS[u]:
                    hi = high_part(pT[:, HI, h, 0:i + 1, i * P:(i + 1) * P],
                                   t_ps[:, c0:c0 + (i + 1) * P].rearrange("p (j t) -> p j t", t=P))
                hi.then_inc(pT_hi, 1)

            def oT_high(b, p, h):
                n = b * NH + 2 * p + h
                act.wait_ge(o_full, n + 1)
                wait_if_any(act, y_full, n - 1)
                high_part(oT[:, HI, h, :], o_ps[:]).then_inc(oT_hi, 1)

            def kq_high(pair, parity, j):
                act.wait_ge(rope_sum, pair * 3 + j + 1)
                high_part(kq[:, parity, j, HI, :], roped[:, (parity * 3 + j) % 2, :]).then_inc(kq_hi, 1)

            def v_high(b, i):
                act.wait_ge(ring_full, ring_base(b) + RING_V + i + 1)
                if i == 0:
                    wait_if_any(act, o_full, b * NH)
                high_part(v_s[:, HI, i, :], ring[(RING_START + RING_V + i) % 2][:]).then_inc(v_hi, 1)

            def xT_high(b_next, unit, k, bank):
                act.wait_ge(ring_full, unit + 1)
                high_part(xnT[:, HI, k, :], bank[:]).then_inc(xT_hi, 1)

            def work(b, first, last):
                for p in range(NP):
                    more = not (last and p == NP - 1)
                    before = not (first and p == 0)
                    pb, pp = (b, p - 1) if p else (b - 1, NP - 1)

                    def kq_next(j):
                        if more:
                            kq_high(b * NP + p + 1, (p + 1) % 2, j)

                    def v_next(i):
                        if p == 0:
                            v_high(b, i)

                    if before:
                        pT_high(pb, pp, 3)
                    exponentials(b, p, 0)
                    if before:
                        pT_high(pb, pp, 4)
                    exponentials(b, p, 1)
                    normalise(b, p, 0)
                    kq_next(0)
                    if before:
                        oT_high(pb, pp, 0)
                    normalise(b, p, 1)
                    exponentials(b, p, 2)
                    if before:
                        oT_high(pb, pp, 1)
                    pT_high(b, p, 0)
                    kq_next(1)
                    normalise(b, p, 2)
                    pT_high(b, p, 1)
                    exponentials(b, p, 3)
                    normalise(b, p, 3)
                    v_next(0)
                    v_next(1)
                    pT_high(b, p, 2)
                    exponentials(b, p, 4)
                    v_next(2)
                    if p == 2 and not last:
                        for k in range(KC):
                            xT_high(b + 1, ring_unit(b, RING_XT + k)[0], k, ring[(RING_START + RING_XT + k) % 2])
                    kq_next(2)
                    v_next(3)
                    normalise(b, p, 4)

            for k in range(KC):
                xT_high(0, k, k, ring[k % 2])
            act.wait_ge(w_loaded[0], 16)
            high_part(wk_s[:, HI], wkv_in[:, 0]).then_inc(w_hi, 1)
            act.wait_ge(w_loaded[1], 16)
            high_part(wq_s[:, HI], wq_in[:]).then_inc(w_hi, 1)
            act.wait_ge(w_loaded[2], 16)
            high_part(wv_s[:, HI], wkv_in[:, 1]).then_inc(w_hi, 1)
            act.wait_ge(w_loaded[3], 16)
            high_part(wo_s[:, HI], wo_in[:]).then_inc(w_hi, 1)
            for j in range(3):
                kq_high(0, 0, j)
            batches(act, work)
            for u in (3, 4):
                pT_high(B - 1, NP - 1, u)
            for h in range(2):
                oT_high(B - 1, NP - 1, h)

        @block.vector
        def _(dve):
            def low_part(out, in_, high):
                return dve.tensor_tensor(out, in_, high.bitcast(F32), ALU.subtract)

            def row_max(b, p, u):
                g = b * (NP * NU) + p * NU + u
                dve.wait_ge(scores_ready, g + 1)
                for n, (h, i, c0) in enumerate(UNITS[u]):
                    mx = dve.tensor_reduce(neg_max[:, u, n:n + 1], s_ps[(p * NU + u) % 2][:, c0:c0 + (i + 1) * P],
                                           AX_X, ALU.max, negate=True)
                mx.then_inc(max_ready, 1)

            def inverse(b, p, u):
                g = b * (NP * NU) + p * NU + u
                n = len(UNITS[u])
                dve.wait_ge(exp_ready, g + 1)
                dve.reciprocal(row_inv[:, u, 0:n], row_sum[:, u, 0:n]).then_inc(inv_ready, 1)

            def pT_low(b, p, u):
                g = b * (NP * NU) + p * NU + u
                dve.wait_ge(pT_hi, g + 1)
                for h, i, c0 in UNITS[u]:
                    cols = slice(i * P, (i + 1) * P)
                    lo = low_part(pT[:, LO, h, 0:i + 1, cols],
                                  t_ps[:, c0:c0 + (i + 1) * P].rearrange("p (j t) -> p j t", t=P),
                                  pT[:, HI, h, 0:i + 1, cols])
                lo.then_inc(pT_lo, 1)

            def oT_low(b, p, h):
                n = b * NH + 2 * p + h
                dve.wait_ge(oT_hi, n + 1)
                low_part(oT[:, LO, h, :], o_ps[:], oT[:, HI, h, :]).then_inc(oT_lo, 1)

            def rotate(pair, j, parity, unit, bank):
                n = pair * 3 + j
                r = (parity * 3 + j) % 2
                t = 0 if j == 0 else 2
                half = D // 2
                dve.wait_ge(ring_full, unit + 1)
                wait_if_any(dve, rope_sum, n - 1)
                dve.tensor_tensor(rope_c[:, r, :], bank[:], tables[:, t, :], ALU.mult)
                dve.tensor_tensor(rope_s[0:half, r, :], bank[half:D], tables[0:half, t + 1, :], ALU.mult)
                dve.tensor_tensor(rope_s[half:D, r, :], bank[0:half], tables[half:D, t + 1, :],
                                  ALU.mult).then_inc(ring_free, 1)

            def v_low(b, i):
                dve.wait_ge(v_hi, b * NT + i + 1)
                low_part(v_s[:, LO, i, :], ring[(RING_START + RING_V + i) % 2][:], v_s[:, HI, i, :]).then_inc(ring_free, 1)

            def xT_low(b_next, k, bank):
                dve.wait_ge(xT_hi, b_next * KC + k + 1)
                low_part(xnT[:, LO, k, :], bank[:], xnT[:, HI, k, :]).then_inc(ring_free, 1)

            def ln_statistics(b_next):
                dve.wait_ge(x_loaded, (b_next + 1) * 16)
                for i in range(NT):
                    st = dve.bn_stats(stats[:, i, :], x_in[:, i, :])
                st.then_inc(ln_stats, 1)
                dve.wait_ge(x_loaded, 16)
                dve.wait_ge(ln_stats, b_next + 1)
                for i in range(NT):
                    ag = dve.bn_aggr(mv[:, i, :], stats[:, i, :])
                ag.then_inc(ln_mv, 1)

            def ln_apply(b_next):
                dve.wait_ge(ln_rstd, b_next + 1)
                for i in range(NT):
                    ap = dve.tensor_scalar(xn[:, i, :], x_in[:, i, :], mv[:, i, 0:1], rstd[:, i:i + 1],
                                           ALU.subtract, ALU.mult)
                ap.then_inc(xn_ready, 1)

            def y_of(i):
                return y_ps[i // 2][:, (i % 2) * C:(i % 2 + 1) * C]

            def y_statistics(b):
                dve.wait_ge(y_full, (b + 1) * NH)
                for i in range(NT):
                    st = dve.bn_stats(y_stats[:, i, :], y_of(i))
                st.then_inc(y_st, 1)
                dve.wait_ge(x_loaded, 16)
                dve.wait_ge(y_st, b + 1)
                for i in range(NT):
                    ag = dve.bn_aggr(y_mv[:, i, :], y_stats[:, i, :])
                ag.then_inc(y_mvs, 1)

            def y_apply(b):
                dve.wait_ge(y_rs, b + 1)
                wait_if_any(dve, x1_stored, b * 16)
                for i in range(NT):
                    ap = dve.tensor_scalar(yn[:, i, :], y_of(i), y_mv[:, i, 0:1], y_rstd[:, i:i + 1],
                                           ALU.subtract, ALU.mult)
                ap.then_inc(yn_ready, 1)

            def x2_statistics(b):
                dve.wait_ge(x1_ready, b + 1)
                for i in range(NT):
                    st = dve.bn_stats(x2_stats[:, i, :], yn[:, i, :])
                st.then_inc(x2_st, 1)
                dve.wait_ge(x_loaded, 16)
                dve.wait_ge(x2_st, b + 1)
                for i in range(NT):
                    ag = dve.bn_aggr(x2_mv[:, i, :], x2_stats[:, i, :])
                ag.then_inc(x2_mvs, 1)

            def x2_apply(b):
                dve.wait_ge(x2_rs, b + 1)
                wait_if_any(dve, xn2_stored, b * 16)
                for i in range(NT):
                    ap = dve.tensor_scalar(xn2_sb[:, i, :], yn[:, i, :], x2_mv[:, i, 0:1], x2_rstd[:, i:i + 1],
                                           ALU.subtract, ALU.mult)
                ap.then_inc(xn2_ready, 1)

            def copy_xn2T(unit0, bank0):
                for k in range(KC):
                    dve.wait_ge(ring_full, unit0 + k + 1)
                    dve.tensor_copy(xn2T[:, k, :], ring[(bank0 + k) % 2][:]).then_inc(ring_free, 1)

            def keep_logits(b, unit0, bank0):
                for n in range(2):
                    dve.wait_ge(ring_full, unit0 + n + 3)
                    tile = b * NT + 2 * n
                    to = logits[:, tile:tile + 2, :] if isinstance(b, int) else logits[:, bass.ds(tile, 2), :]
                    dve.tensor_scalar(to, ring[(bank0 + n) % 2][:, 0:2 * NE].rearrange("p (i e) -> p i e", e=NE),
                                      1.0, None, ALU.mult).then_inc(ring_free, 1)

            def work(b, first, last):
                router = RING_ROUTER_LAST if last else RING_ROUTER
                for p in range(NP):
                    more = not (last and p == NP - 1)
                    before = not (first and p == 0)
                    pb, pp = (b, p - 1) if p else (b - 1, NP - 1)

                    def rotate_next(j):
                        if more:
                            rotate(b * NP + p + 1, j, (p + 1) % 2, *ring_unit(b, RING_ROPE[p] + j))

                    def v_next(i):
                        if p == 0:
                            v_low(b, i)

                    row_max(b, p, 0)
                    if before:
                        pT_low(pb, pp, 3)
                    rotate_next(0)
                    if before:
                        pT_low(pb, pp, 4)
                    row_max(b, p, 1)
                    inverse(b, p, 0)
                    rotate_next(1)
                    inverse(b, p, 1)
                    if before:
                        oT_low(pb, pp, 0)
                    row_max(b, p, 2)
                    if p == 1 and not first:
                        y_apply(b - 1)
                    if before:
                        oT_low(pb, pp, 1)
                    inverse(b, p, 2)
                    pT_low(b, p, 0)
                    row_max(b, p, 3)
                    pT_low(b, p, 1)
                    if p == 2 and not last:
                        ln_apply(b + 1)
                    if p == 3 and not first:
                        x2_apply(b - 1)
                    inverse(b, p, 3)
                    rotate_next(2)
                    v_next(0)
                    v_next(1)
                    if p == 3 and not first:
                        copy_xn2T(ring_base(b) + router, RING_START + router)
                    row_max(b, p, 4)
                    pT_low(b, p, 2)
                    v_next(2)
                    inverse(b, p, 4)
                    if p == 2 and not last:
                        for k in range(KC):
                            xT_low(b + 1, k, ring[(RING_START + RING_XT + k) % 2])
                    v_next(3)
                    if p == 0 and not first:
                        y_statistics(b - 1)
                    if p == 1 and not last:
                        ln_statistics(b + 1)
                    if p == 2 and not first:
                        x2_statistics(b - 1)
                    if p == 3 and not first:
                        keep_logits(b - 1, ring_base(b) + router, RING_START + router)

            ln_statistics(0)
            ln_apply(0)
            for k in range(KC):
                xT_low(0, k, ring[k % 2])
            dve.wait_ge(consts_loaded, 48)
            dve.tensor_copy(ident_bf[:], mask_in[:, 0, :]).then_inc(masks_ready, 1)
            dve.tensor_copy(causal_bf[:], mask_in[:, 1, :]).then_inc(masks_ready, 1)
            for n, (split, whole) in enumerate(((wk_s, wkv_in[:, 0]), (wq_s, wq_in[:]), (wv_s, wkv_in[:, 1]),
                                                (wo_s, wo_in[:]))):
                dve.wait_ge(w_hi, n + 1)
                low_part(split[:, LO], whole, split[:, HI]).then_inc(w_lo, 1)
            for j in range(3):
                rotate(0, j, 0, KC + j, ring[(KC + j) % 2])
            batches(dve, work)
            for u in (3, 4):
                pT_low(B - 1, NP - 1, u)
            for h in range(2):
                oT_low(B - 1, NP - 1, h)
            y_statistics(B - 1)
            y_apply(B - 1)
            x2_statistics(B - 1)
            x2_apply(B - 1)
            end = ring_base(B - 1) + RING_ROUTER_END
            copy_xn2T(end, RING_START + RING_ROUTER_END)
            keep_logits(B - 1, end, RING_START + RING_ROUTER_END)

        @block.gpsimd
        def _(pool):
            def inverse_std(count, mv_, vare_, rstd_, mv_ready, vare_ready, rstd_ready):
                pool.wait_ge(mv_ready, count)
                pool.tensor_tensor(vare_[:], mv_[:, :, 1], eps_t[:], ALU.add).then_inc(vare_ready, 1)
                pool.wait_ge(vare_ready, count)
                pool.tensor_tensor(rstd_[:], vare_[:], mhalf_t[:], ALU.pow).then_inc(rstd_ready, 1)

            def add_products(pair, j, parity, unit):
                n = pair * 3 + j
                r = (parity * 3 + j) % 2
                pool.wait_ge(ring_free, unit + 1)
                wait_if_any(pool, kq_lo, n - 1)
                pool.tensor_tensor(roped[:, r, :], rope_c[:, r, :], rope_s[:, r, :], ALU.add).then_inc(rope_sum, 1)

            def kq_low(pair, j, parity):
                r = (parity * 3 + j) % 2
                pool.wait_ge(kq_hi, pair * 3 + j + 1)
                pool.tensor_tensor(kq[:, parity, j, LO, :], roped[:, r, :], kq[:, parity, j, HI, :].bitcast(F32),
                                   ALU.subtract).then_inc(kq_lo, 1)

            def pair_work(pair, parity, unit0):
                for j in range(3):
                    add_products(pair, j, parity, unit0 + j)
                    kq_low(pair, j, parity)

            def add_residual(b):
                pool.wait_ge(yn_ready, b + 1)
                pool.wait_ge(res_loaded, (b + 1) * 16)
                pool.tensor_tensor(yn[:], yn[:], x_res[:], ALU.add).then_inc(x1_ready, 1)

            def work(b, first, last):
                for p in range(NP):
                    if not (last and p == NP - 1):
                        pair_work(b * NP + p + 1, (p + 1) % 2, ring_unit(b, RING_ROPE[p])[0])
                    if p == 0 and not first:
                        inverse_std(b, y_mv, y_vare, y_rstd, y_mvs, y_ve, y_rs)
                    if p == 1 and not first:
                        add_residual(b - 1)
                    if p == 1 and not last:
                        inverse_std(b + 2, mv, vare, rstd, ln_mv, ln_vare, ln_rstd)
                    if p == 2 and not first:
                        inverse_std(b, x2_mv, x2_vare, x2_rstd, x2_mvs, x2_ve, x2_rs)

            pool.memset(filler[:], 0.0).then_inc(filler_ready, 1)
            pool.memset(eps_t[:], EPS)
            pool.memset(mhalf_t[:], -0.5).then_inc(pool_consts, 1)
            pool.wait_ge(pool_consts, 1)
            inverse_std(1, mv, vare, rstd, ln_mv, ln_vare, ln_rstd)
            pair_work(0, 0, KC)
            batches(pool, work)
            inverse_std(B, y_mv, y_vare, y_rstd, y_mvs, y_ve, y_rs)
            add_residual(B - 1)
            inverse_std(B, x2_mv, x2_vare, x2_rstd, x2_mvs, x2_ve, x2_rs)


def shared_ffn(nc, ctx, name, xn2, shared_out, w1_s, w2_s, w3_s, ident, first_block, blocks):
    units = HID // P

    def sb(what, shape, dt=F32):
        return ctx.enter_context(nc.sbuf_tensor(f"{name}_{what}", shape, dt))

    def ps(what):
        return ctx.enter_context(nc.psum_tensor(f"{name}_{what}", [P, T], F32))

    def sem(what):
        return ctx.enter_context(nc.semaphore(f"{name}_{what}"))

    x_in = sb("x_in", [P, NT, C])
    xT = sb("xT", [P, 2, KC, T], F32R)
    gate = sb("gate", [P, 2, T])
    hidden = sb("hidden", [P, 2, T])
    h_s = sb("h_split", [P, 2, 2, T], F32R)
    out = sb("out", [P, NT, C])
    h1_ps = [ps("h1_ps0"), ps("h1_ps1")]
    h2_ps = [ps("h2_ps0"), ps("h2_ps1")]
    x_ps = [ps("x_ps0"), ps("x_ps1")]
    y_ps = [ps("y_ps0"), ps("y_ps1")]
    x_loaded, x_turned, xT_hi, xT_lo = sem("x_loaded"), sem("x_turned"), sem("xT_hi"), sem("xT_lo")
    h1_full, h2_full, gate_ready, hidden_ready = sem("h1_full"), sem("h2_full"), sem("gate_ready"), sem("hidden_ready")
    h_hi, h_lo, y_full, out_ready, stored = sem("h_hi"), sem("h_lo"), sem("y_full"), sem("out_ready"), sem("stored")

    x_rows = xn2.rearrange("b (i p) c -> b p i c", p=P)
    out_rows = shared_out.rearrange("b (i p) c -> b p i c", p=P)

    class work:

        x_psum = x_ps
        output = out
        first_gates = gate

        def load(sp, j):
            wait_if_any(sp, x_turned, j * KC)
            sp.dma_start(x_in[:], rows_of(x_rows, first_block + j)).then_inc(x_loaded, 16)

        def store(sp, j):
            sp.wait_ge(out_ready, (j + 1) * 2)
            sp.dma_start(rows_of(out_rows, first_block + j), out[:]).then_inc(stored, 16)

        def turn(pe, j):
            pe.wait_ge(x_loaded, (j + 1) * 16)
            wait_if_any(pe, xT_lo, j * KC)
            for k in range(KC):
                for i in range(NT):
                    mm = pe.transpose(x_ps[k][:, i * P:(i + 1) * P], x_in[:, i, k * P:(k + 1) * P], ident)
                mm.then_inc(x_turned, 1)

        def tensor(pe, j, last):
            def up(m):
                if m == 0:
                    pe.wait_ge(xT_lo, (j + 1) * KC)
                wait_if_any(pe, hidden_ready, j * units + m - 1)
                for w, bank, full in ((w1_s, h1_ps[m % 2], h1_full), (w2_s, h2_ps[m % 2], h2_full)):
                    n = 0
                    for a, c in PASSES:
                        for k in range(KC):
                            mm = pe.matmul(bank[:], w[:, a, k, m * P:(m + 1) * P], xT[:, c, k, :],
                                           start=(n == 0), stop=(n == 3 * KC - 1))
                            n += 1
                    mm.then_inc(full, 1)

            def down(m):
                pe.wait_ge(h_lo, j * units + m + 1)
                if m == 0:
                    wait_if_any(pe, out_ready, j * 2)
                for i in range(NT):
                    for n, (a, c) in enumerate(PASSES):
                        mm = pe.matmul(y_ps[i // 2][:, (i % 2) * C:(i % 2 + 1) * C],
                                       h_s[:, m % 2, a, i * P:(i + 1) * P], w3_s[:, c, m, :],
                                       start=(m == 0 and n == 0 and i % 2 == 0),
                                       stop=(m == units - 1 and n == 2), skip_group_check=True)
                mm.then_inc(y_full, 1)

            for m in range(units):
                up(m)
                if m >= 1:
                    down(m - 1)
            if not last:
                work.turn(pe, j + 1)
            down(units - 1)

        def split_x_high(act, j):
            for k in range(KC):
                act.wait_ge(x_turned, j * KC + k + 1)
                if k == 0:
                    wait_if_any(act, h2_full, j * units)
                act.activation(xT[:, HI, k, :], x_ps[k][:], ACT.Copy).then_inc(xT_hi, 1)

        def scalar(act, j, last, between=lambda m: None):
            for m in range(units):
                between(m)
                n = j * units + m
                act.wait_ge(h1_full, n + 1)
                wait_if_any(act, hidden_ready, n - 1)
                act.activation(gate[:, m % 2, :], h1_ps[m % 2][:], ACT.Silu).then_inc(gate_ready, 1)
                act.wait_ge(hidden_ready, n + 1)
                wait_if_any(act, y_full, n - 1)
                act.activation(h_s[:, m % 2, HI, :], hidden[:, m % 2, :], ACT.Copy).then_inc(h_hi, 1)
            if not last:
                work.split_x_high(act, j + 1)
            act.wait_ge(y_full, (j + 1) * units)
            wait_if_any(act, stored, j * 16)
            for n in range(2):
                act.activation(out[:, 2 * n:2 * n + 2, :],
                               y_ps[n][:].rearrange("p (i c) -> p i c", c=C), ACT.Copy).then_inc(out_ready, 1)

        def split_x_low(dve, j):
            for k in range(KC):
                dve.wait_ge(xT_hi, j * KC + k + 1)
                dve.tensor_tensor(xT[:, LO, k, :], x_ps[k][:], xT[:, HI, k, :].bitcast(F32),
                                  ALU.subtract).then_inc(xT_lo, 1)

        def vector(dve, j, last, between=lambda m: None):
            for m in range(units):
                between(m)
                n = j * units + m
                dve.wait_ge(h2_full, n + 1)
                dve.wait_ge(gate_ready, n + 1)
                wait_if_any(dve, h_lo, n - 1)
                dve.tensor_tensor(hidden[:, m % 2, :], h2_ps[m % 2][:], gate[:, m % 2, :],
                                  ALU.mult).then_inc(hidden_ready, 1)
                dve.wait_ge(h_hi, n + 1)
                dve.tensor_tensor(h_s[:, m % 2, LO, :], hidden[:, m % 2, :], h_s[:, m % 2, HI, :].bitcast(F32),
                                  ALU.subtract).then_inc(h_lo, 1)
            if not last:
                work.split_x_low(dve, j + 1)

        def all_stored(engine):
            engine.wait_ge(stored, 16 * blocks)

        def wait_stored(engine, j):
            engine.wait_ge(stored, 16 * (j + 1))

    return work


def peeled(engine, count, slot_work):
    slot_work(0, True, False)
    with engine.Fori(1, count - 1) as j:
        slot_work(j, False, False)
    slot_work(count - 1, False, True)


def split_weights(sem, loads, stage):
    loaded = [sem("weights_loaded0"), sem("weights_loaded1")]
    high, low = sem("weights_high"), sem("weights_low")

    def load(sp):
        for n, (src, split, shape) in enumerate(loads):
            wait_if_any(sp, low, n - 1)
            sp.dma_start(shape(stage[:, n % 2, :]), src).then_inc(loaded[n % 2], 16)

    def make_high(act, numbers):
        for n in numbers:
            src, split, shape = loads[n]
            act.wait_ge(loaded[n % 2], 16 * (n // 2 + 1))
            act.activation(split(HI), shape(stage[:, n % 2, :]), ACT.Copy).then_inc(high, 1)

    def make_low(dve, numbers):
        for n in numbers:
            src, split, shape = loads[n]
            dve.wait_ge(high, n + 1)
            dve.tensor_tensor(split(LO), shape(stage[:, n % 2, :]), split(HI).bitcast(F32),
                              ALU.subtract).then_inc(low, 1)

    return load, make_high, make_low, low


def routing_phase(nc, xn2, xs, logits, expert_bias, lanes, masks, shared_w, expert_w, shared_out,
                  w1_s, w2_s, w3_s, w12_s, we3_s, ident, dest, gates, tile_expert):
    half = BLOCKS // 2
    with ExitStack() as ctx:
        def sb(name, shape, dt=F32):
            return ctx.enter_context(nc.sbuf_tensor(name, shape, dt))

        def sem(name):
            return ctx.enter_context(nc.semaphore(name))

        shared = shared_ffn(nc, ctx, "sh0", xn2, shared_out, w1_s, w2_s, w3_s, ident, 0, half)
        stage = sb("stage", [P, 2, 1024])
        x_tiles = sb("x_tiles", [P, 2, NT, C])
        dest_now = sb("dest_now", [P, 2, NT, TOP_K], mybir.dt.int32)
        room = x_tiles[:].rearrange("p a i c -> p (a i c)").rearrange("p (n t e) -> p n t e", n=4, e=NE)
        prob, value, first, second = (room[:, n] for n in range(4))
        work_t, slot = (shared.output[:].rearrange("p i c -> p (i c)").rearrange(
            "p (n t e) -> p n t e", n=2, e=NE)[:, n] for n in range(2))
        best = sb("route_best", [P, TOKEN_TILES])
        chosen = sb("route_chosen", [P, TOKEN_TILES, NE], BF16)
        sums = [sb("route_sums0", [P, 2 * TOKEN_TILES, NE]), sb("route_sums1", [P, 2 * TOKEN_TILES, NE])]
        bias = sb("route_bias", [P, NE])
        lane = sb("route_lane", [P, NE])
        upper = sb("route_upper", [P, P], BF16)
        ones = sb("route_ones", [P, P], BF16)
        mask_f = sb("route_mask", [P, P])
        count_f = sb("route_count", [P, NE])
        count_i = sb("route_count_i", [P, 2, NE], mybir.dt.int32)
        tiles_f = sb("route_tiles", [P, NE])
        ends = [sb("route_ends0", [P, 2 * NE]), sb("route_ends1", [P, 2 * NE])]
        base = sb("route_base", [P, NE])
        picked = sb("route_picked", [P, TOKEN_TILES])
        tile_no = sb("route_tile_no", [1, TILES])
        tile_acc = shared.first_gates[0:1, :, 0:TILES]
        rank_ps, total_ps = shared.x_psum

        small_loaded = sem("small_loaded")
        exp_done = sem("exp_done")
        step_done = sem("step_done")
        chosen_ready = sem("chosen_ready")
        rank_ready = sem("rank_ready")
        routed = sem("routed")
        rows_loaded = [sem("rows_loaded0"), sem("rows_loaded1")]
        dest_copied = [sem("dest_copied0"), sem("dest_copied1")]
        rows_sent = [sem("rows_sent0"), sem("rows_sent1")]

        x_rows = xn2.rearrange("b (i p) c -> b p i c", p=P)
        loads = [*shared_w, *expert_w]
        load_w, split_high, split_low, w_low = split_weights(sem, loads, stage)

        def expert_loads(m):
            n = len(expert_w) // (HID // P)
            return range(len(shared_w) + m * n, len(shared_w) + (m + 1) * n)

        block = ctx.enter_context(nc.Block())

        @block.sync
        def _(sp):
            sp.dma_start(bias[:], expert_bias.partition_broadcast(P)).then_inc(small_loaded, 16)
            sp.dma_start(lane[:], lanes[0:P * NE].rearrange("(p e) -> p e", e=NE)).then_inc(small_loaded, 16)
            sp.dma_start(tile_no[:], lanes[P * NE:P * NE + TILES].rearrange("(p n) -> p n", p=1)).then_inc(small_loaded, 16)
            sp.dma_start(mask_f[:], masks[2]).then_inc(small_loaded, 16)
            shared.load(sp, 0)
            load_w(sp)

            def work(j, first_, last):
                for q in range(2):
                    if first_:
                        sp.wait_ge(routed, 1)
                    else:
                        sp.wait_ge(rows_sent[q], j * 16 * NT * TOP_K)
                    sp.dma_start(x_tiles[:, q], rows_of(x_rows, 2 * j + q)).then_inc(rows_loaded[q], 16)
                if not last:
                    shared.load(sp, j + 1)
                shared.store(sp, j)

            peeled(sp, half, work)
            shared.all_stored(sp)
            for q in range(2):
                sp.wait_ge(rows_sent[q], half * 16 * NT * TOP_K)

        @block.gpsimd
        def _(pool):
            pool.wait_ge(routed, 1)

            def work(j, nth, first_):
                for q in range(2):
                    tile = (2 * j + q) * NT
                    now = dest[:, tile:tile + NT, :] if isinstance(j, int) else dest[:, bass.ds(tile, NT), :]
                    if not first_:
                        pool.wait_ge(small_loaded, 64)
                        pool.wait_ge(rows_sent[q], j * 16 * NT * TOP_K)
                    pool.wait_ge(rows_loaded[q], nth * 16)
                    pool.tensor_copy(dest_now[:, q], now).then_inc(dest_copied[q], 1)
                    pool.wait_ge(small_loaded, 64)
                    pool.wait_ge(dest_copied[q], nth)
                    for i in range(NT):
                        for k in range(TOP_K):
                            pool.indirect_dma_start(
                                xs[:, :], bass.IndirectOffsetOnAxis(ap=dest_now[:, q, i, k:k + 1], axis=0),
                                x_tiles[:, q, i, :], None).then_inc(rows_sent[q], 16)

            work(0, 1, True)
            with pool.Fori(2, half + 1) as nth:
                work(nth - 1, nth, False)

        @block.tensor
        def _(pe):
            pe.wait_ge(chosen_ready, 1)
            rows = chosen[:].rearrange("p t e -> p (t e)")
            pe.matmul(rank_ps[:], upper[:], rows, start=True, stop=True)
            pe.matmul(total_ps[:], ones[:], rows, start=True, stop=True).then_inc(rank_ready, 1)
            pe.wait_ge(routed, 1)
            shared.turn(pe, 0)
            pe.wait_ge(w_low, len(shared_w))
            peeled(pe, half, lambda j, first_, last: shared.tensor(pe, j, last))

        @block.scalar
        def _(act):
            act.activation(prob, logits[:], ACT.Exp, scale=-1.0).then_inc(exp_done, 1)
            split_high(act, range(len(shared_w)))
            shared.split_x_high(act, 0)
            peeled(act, half, lambda j, first_, last: shared.scalar(
                act, j, last, lambda m: split_high(act, expert_loads(m) if first_ else ())))

        @block.vector
        def _(dve):
            steps = [0]

            def step(instruction):
                steps[0] += 1
                instruction.then_inc(step_done, 1)
                dve.wait_ge(step_done, steps[0])

            by_tile = [P, TOKEN_TILES, NE]

            def over_tiles(a):
                return a.unsqueeze(1).broadcast_to(by_tile)

            def over_experts(a):
                return a.unsqueeze(2).broadcast_to(by_tile)

            dve.wait_ge(small_loaded, 64)
            dve.tensor_copy(upper[:], mask_f[:])
            dve.memset(ones[:], 1.0)
            dve.memset(sums[0][:, 0:TOKEN_TILES, :], 0.0)
            dve.memset(sums[1][:, 0:TOKEN_TILES, :], 0.0)
            dve.memset(ends[0][:, 0:NE], 0.0)
            dve.memset(ends[1][:, 0:NE], 0.0)
            dve.wait_ge(exp_done, 1)
            step(dve.tensor_scalar(prob, prob, 1.0, None, ALU.add))
            step(dve.reciprocal(prob, prob))
            step(dve.tensor_tensor(value, prob, over_tiles(bias[:]), ALU.add))

            def pick(out):
                step(dve.tensor_reduce(best[:], value, AX_X, ALU.max))
                step(dve.tensor_tensor(work_t, value, over_experts(best[:]), ALU.is_equal))
                step(dve.tensor_tensor(work_t, work_t, over_tiles(lane[:]), ALU.mult))
                step(dve.tensor_reduce(best[:], work_t, AX_X, ALU.max))
                step(dve.tensor_tensor(out, work_t, over_experts(best[:]), ALU.is_equal))

            pick(first)
            step(dve.scalar_tensor_tensor(value, first, TAKEN, value, ALU.mult, ALU.add))
            pick(second)
            dve.tensor_tensor(chosen[:], first, second, ALU.add).then_inc(chosen_ready, 1)
            dve.wait_ge(rank_ready, 1)
            step(dve.tensor_copy(sums[0][:, TOKEN_TILES:, :], total_ps[:].rearrange("p (t e) -> p t e", e=NE)))
            n, reach = 0, 1
            while reach < TOKEN_TILES:
                src, dst = sums[n % 2], sums[(n + 1) % 2]
                step(dve.tensor_tensor(dst[:, TOKEN_TILES:, :], src[:, TOKEN_TILES:, :],
                                       src[:, TOKEN_TILES - reach:2 * TOKEN_TILES - reach, :], ALU.add))
                n, reach = n + 1, 2 * reach
            upto = sums[n % 2]
            step(dve.tensor_scalar(count_i[:, 0, :], upto[:, 2 * TOKEN_TILES - 1, :], float(P - 1), None, ALU.add))
            step(dve.tensor_scalar(count_i[:, 1, :], count_i[:, 0, :], P.bit_length() - 1, None,
                                   ALU.logical_shift_right))
            step(dve.tensor_copy(tiles_f[:], count_i[:, 1, :]))
            step(dve.tensor_copy(ends[0][:, NE:], tiles_f[:]))
            n, reach = 0, 1
            while reach < NE:
                src, dst = ends[n % 2], ends[(n + 1) % 2]
                step(dve.tensor_tensor(dst[:, NE:], src[:, NE:], src[:, NE - reach:2 * NE - reach], ALU.add))
                n, reach = n + 1, 2 * reach
            end = ends[n % 2][:, NE:]
            step(dve.tensor_tensor(base[:], end, tiles_f[:], ALU.subtract))
            step(dve.tensor_tensor(slot, upto[:, TOKEN_TILES:, :],
                                   total_ps[:].rearrange("p (t e) -> p t e", e=NE), ALU.subtract))
            step(dve.tensor_tensor(slot, slot, rank_ps[:].rearrange("p (t e) -> p t e", e=NE), ALU.add))
            step(dve.tensor_scalar(base[:], base[:], float(P), None, ALU.mult))
            step(dve.tensor_tensor(slot, slot, over_tiles(base[:]), ALU.add))
            for k, one_hot in enumerate((first, second)):
                step(dve.tensor_tensor(work_t, one_hot, slot, ALU.mult))
                step(dve.tensor_reduce(picked[:], work_t, AX_X, ALU.add))
                step(dve.tensor_copy(dest[:, :, k], picked[:]))
                step(dve.tensor_tensor(work_t, one_hot, prob, ALU.mult))
                step(dve.tensor_reduce(gates[:, :, k], work_t, AX_X, ALU.add))
            step(dve.memset(tile_acc[:, 0, :], 0.0))
            for e in range(NE - 1):
                step(dve.scalar_tensor_tensor(tile_acc[:, (e + 1) % 2, :], tile_no[:], end[0:1, e:e + 1],
                                              tile_acc[:, e % 2, :], ALU.is_ge, ALU.add))
            dve.tensor_copy(tile_expert[:], tile_acc[:, (NE - 1) % 2, :]).then_inc(routed, 1)

            split_low(dve, range(len(shared_w)))
            shared.split_x_low(dve, 0)
            peeled(dve, half, lambda j, first_, last: shared.vector(
                dve, j, last, lambda m: split_low(dve, expert_loads(m) if first_ else ())))


def experts_phase(nc, xs, ys, w12_s, we3_s, ident, tile_expert):
    with ExitStack() as ctx:
        def sb(name, shape, dt=F32):
            return ctx.enter_context(nc.sbuf_tensor(name, shape, dt))

        def ps(name, cols):
            return [ctx.enter_context(nc.psum_tensor(f"{name}{n}", [P, T], F32))[:, 0:cols] for n in range(2)]

        def sem(name):
            return ctx.enter_context(nc.semaphore(name))

        RING = 4
        x_t = sb("e_x", [P, RING, C])
        xT = sb("e_xT", [P, 2, 2, KC, P], F32R)
        gate = sb("e_gate", [P, 2, HE])
        hidden = sb("e_hidden", [P, 2, HE])
        hT = sb("e_hT", [P, 2, 2, KH, P], F32R)
        y_t = sb("e_y", [P, RING, C])
        x_ps, h_ps, hT_ps, y_ps = ps("e_x_ps", C), ps("e_h_ps", 2 * HE), ps("e_hT_ps", HE), ps("e_y_ps", C)

        loaded = [sem(f"e_loaded{n}") for n in range(RING)]
        stored = [sem(f"e_stored{n}") for n in range(RING)]
        x_turned, x_hi, x_lo = sem("e_x_turned"), sem("e_x_hi"), sem("e_x_lo")
        h_full, gate_ready, hidden_ready = sem("e_h_full"), sem("e_gate_ready"), sem("e_hidden_ready")
        h_turned, h_hi, h_lo = sem("e_h_turned"), sem("e_h_hi"), sem("e_h_lo")
        y_full, y_ready = sem("e_y_full"), sem("e_y_ready")

        xs_tiles = xs.rearrange("(n p) c -> n p c", p=P)
        ys_tiles = ys.rearrange("(n p) c -> n p c", p=P)

        def tile_of(tiles, n):
            return tiles[n] if isinstance(n, int) else tiles[bass.ds(n, 1)].rearrange("n p c -> (n p) c")

        def exists(n):
            return not isinstance(n, int) or 0 <= n < TILES

        def tiles(engine, step):
            for r in range(RING):
                step(r, r)
            with engine.Fori(1, TILES // RING - 1) as g:
                for r in range(RING):
                    step(g * RING + r, r)
            for r in range(RING + 2):
                step(TILES - RING + r, r % RING)

        block = ctx.enter_context(nc.Block())

        @block.sync
        def _(sp):
            for r in range(RING - 1):
                sp.dma_start(x_t[:, r], tile_of(xs_tiles, r)).then_inc(loaded[r], 16)

            def step(n, r):
                if exists(n + RING - 1):
                    wait_if_any(sp, x_turned, n)
                    sp.dma_start(x_t[:, (r + RING - 1) % RING], tile_of(xs_tiles, n + RING - 1)).then_inc(
                        loaded[(r + RING - 1) % RING], 16)
                if exists(n - 2):
                    sp.wait_ge(y_ready, n - 1)
                    sp.dma_start(tile_of(ys_tiles, n - 2), y_t[:, (r - 2) % RING]).then_inc(stored[(r - 2) % RING], 16)

            tiles(sp, step)
            for r in range(RING):
                sp.wait_ge(stored[r], TILES // RING * 16)

        @block.tensor
        def _(pe):
            def turn_x(n, r, group):
                pe.wait_ge(loaded[r], group * 16)
                wait_if_any(pe, x_lo, n - 1)
                for k in range(KC):
                    mm = pe.transpose(x_ps[r % 2][:, k * P:(k + 1) * P], x_t[:, r, k * P:(k + 1) * P], ident)
                mm.then_inc(x_turned, 1)

            def expert_of(n):
                at = tile_expert[0:1, n:n + 1] if isinstance(n, int) else tile_expert[0:1, bass.ds(n, 1)]
                return pe.value_load(at, min_val=0, max_val=NE - 1)

            def up(n, r):
                e = expert_of(n)
                pe.wait_ge(x_lo, n + 1)
                wait_if_any(pe, hidden_ready, n - 1)
                m = 0
                for a, c in PASSES:
                    for k in range(KC):
                        mm = pe.matmul(h_ps[r % 2], xT[:, r % 2, a, k, :],
                                       w12_s[:, bass.ds(e, 1), c, k, :].rearrange("p e n -> p (e n)"),
                                       start=(m == 0), stop=(m == 3 * KC - 1))
                        m += 1
                mm.then_inc(h_full, 1)

            def turn_h(n, r):
                pe.wait_ge(hidden_ready, n + 1)
                wait_if_any(pe, h_lo, n - 1)
                for k in range(KH):
                    mm = pe.transpose(hT_ps[r % 2][:, k * P:(k + 1) * P], hidden[:, r % 2, k * P:(k + 1) * P], ident)
                mm.then_inc(h_turned, 1)

            def down(n, r):
                e = expert_of(n)
                pe.wait_ge(h_lo, n + 1)
                wait_if_any(pe, y_ready, n - 1)
                m = 0
                for a, c in PASSES:
                    for k in range(KH):
                        mm = pe.matmul(y_ps[r % 2], hT[:, r % 2, a, k, :],
                                       we3_s[:, bass.ds(e, 1), c, k, :].rearrange("p e n -> p (e n)"),
                                       start=(m == 0), stop=(m == 3 * KH - 1))
                        m += 1
                mm.then_inc(y_full, 1)

            turn_x(0, 0, 1)

            def step(n, r):
                if exists(n + 1):
                    turn_x(n + 1, (r + 1) % RING, group_of[0] + 1 + (r + 1 == RING))
                if exists(n):
                    up(n, r)
                if exists(n - 1):
                    turn_h(n - 1, (r - 1) % RING)
                if exists(n - 2):
                    down(n - 2, (r - 2) % RING)

            group_of = [0]
            for r in range(RING):
                step(r, r)
            with pe.Fori(1, TILES // RING - 1) as g:
                group_of[0] = g
                for r in range(RING):
                    step(g * RING + r, r)
            group_of[0] = TILES // RING - 1
            for r in range(RING + 2):
                step(TILES - RING + r, r % RING)

        @block.scalar
        def _(act):
            def step(n, r):
                if exists(n + 1):
                    act.wait_ge(x_turned, n + 2)
                    wait_if_any(act, h_full, n)
                    act.activation(xT[:, (r + 1) % 2, HI].rearrange("p k t -> p (k t)"), x_ps[(r + 1) % 2],
                                   ACT.Copy).then_inc(x_hi, 1)
                if exists(n):
                    act.wait_ge(h_full, n + 1)
                    wait_if_any(act, hidden_ready, n - 1)
                    act.activation(gate[:, r % 2, :], h_ps[r % 2][:, 0:HE], ACT.Silu).then_inc(gate_ready, 1)
                if exists(n - 1):
                    act.wait_ge(h_turned, n)
                    wait_if_any(act, y_full, n - 2)
                    act.activation(hT[:, (r - 1) % 2, HI].rearrange("p k t -> p (k t)"), hT_ps[(r - 1) % 2],
                                   ACT.Copy).then_inc(h_hi, 1)
                if exists(n - 2):
                    act.wait_ge(y_full, n - 1)
                    if not isinstance(n, int) or n - 2 >= RING:
                        act.wait_ge(stored[(r - 2) % RING], group_of[0] * 16 - (16 if r < 2 else 0))
                    act.activation(y_t[:, (r - 2) % RING, :], y_ps[r % 2], ACT.Copy).then_inc(y_ready, 1)

            group_of = [0]
            act.wait_ge(x_turned, 1)
            act.activation(xT[:, 0, HI].rearrange("p k t -> p (k t)"), x_ps[0], ACT.Copy).then_inc(x_hi, 1)
            for r in range(RING):
                step(r, r)
            with act.Fori(1, TILES // RING - 1) as g:
                group_of[0] = g
                for r in range(RING):
                    step(g * RING + r, r)
            for r in range(RING + 2):
                group_of[0] = TILES // RING - 1 + r // RING
                step(TILES - RING + r, r % RING)

        @block.vector
        def _(dve):
            def x_low(n, r):
                dve.wait_ge(x_hi, n + 1)
                dve.tensor_tensor(xT[:, r % 2, LO].rearrange("p k t -> p (k t)"), x_ps[r % 2],
                                  xT[:, r % 2, HI].rearrange("p k t -> p (k t)").bitcast(F32),
                                  ALU.subtract).then_inc(x_lo, 1)

            def step(n, r):
                if exists(n + 1):
                    x_low(n + 1, r + 1)
                if exists(n):
                    dve.wait_ge(gate_ready, n + 1)
                    wait_if_any(dve, h_turned, n - 1)
                    dve.tensor_tensor(hidden[:, r % 2, :], h_ps[r % 2][:, HE:2 * HE], gate[:, r % 2, :],
                                      ALU.mult).then_inc(hidden_ready, 1)
                if exists(n - 1):
                    dve.wait_ge(h_hi, n)
                    dve.tensor_tensor(hT[:, (r - 1) % 2, LO].rearrange("p k t -> p (k t)"), hT_ps[(r - 1) % 2],
                                      hT[:, (r - 1) % 2, HI].rearrange("p k t -> p (k t)").bitcast(F32),
                                      ALU.subtract).then_inc(h_lo, 1)

            x_low(0, 0)
            tiles(dve, step)


def combine_phase(nc, xn2, x1, ys, shared_out, w1_s, w2_s, w3_s, ident, dest, gates, out):
    half = BLOCKS // 2
    with ExitStack() as ctx:
        def sb(name, shape, dt=F32):
            return ctx.enter_context(nc.sbuf_tensor(name, shape, dt))

        def sem(name):
            return ctx.enter_context(nc.semaphore(name))

        shared = shared_ffn(nc, ctx, "sh1", xn2, shared_out, w1_s, w2_s, w3_s, ident, half, half)
        from_experts = sb("c_experts", [P, 2, NT, TOP_K, C])
        from_shared = sb("c_shared", [P, 2, NT, C])
        residual = sb("c_residual", [P, 2, NT, C])
        dest_now = sb("c_dest", [P, 2, NT, TOP_K], mybir.dt.int32)
        gate_now = sb("c_gate", [P, 2, NT, TOP_K])
        stats = sb("c_stats", [P, NT, 6])
        mv = sb("c_mv", [P, NT, 2])
        vare = sb("c_vare", [P, NT])
        rstd = sb("c_rstd", [P, NT])
        eps_t = sb("c_eps", [P, NT])
        mhalf_t = sb("c_mhalf", [P, NT])

        gathered = [sem("c_gathered0"), sem("c_gathered1")]
        loaded = [sem("c_loaded0"), sem("c_loaded1")]
        numbers_ready = [sem("c_numbers0"), sem("c_numbers1")]
        summed = sem("c_summed")
        added = sem("c_added")
        gates_ready = sem("c_gates")
        stat_ready = sem("c_stat")
        mv_ready = sem("c_mv_ready")
        vare_ready = sem("c_vare_ready")
        rstd_ready = sem("c_rstd_ready")
        normed = sem("c_normed")
        out_ready = sem("c_out_ready")
        out_stored = [sem("c_stored0"), sem("c_stored1")]
        consts = sem("c_consts")

        def rows(a):
            return a.rearrange("b (i p) c -> b p i c", p=P)

        block = ctx.enter_context(nc.Block())

        def blocks_of(j):
            return ((2 * j + q, q) for q in range(2))

        @block.sync
        def _(sp):
            shared.load(sp, 0)

            def work(j, first_, last):
                for c, q in blocks_of(j):
                    if not first_:
                        sp.wait_ge(out_stored[q], j * 16)
                    sp.dma_start(residual[:, q], rows_of(rows(x1), c)).then_inc(loaded[q], 16)
                    if last and q == 0:
                        shared.store(sp, j)
                        shared.wait_stored(sp, j)
                    sp.dma_start(from_shared[:, q], rows_of(rows(shared_out), c)).then_inc(loaded[q], 16)
                if not last:
                    shared.load(sp, j + 1)
                    shared.store(sp, j)
                    shared.wait_stored(sp, j)
                for c, q in blocks_of(j):
                    sp.wait_ge(out_ready, c + 1)
                    sp.dma_start(rows_of(rows(out), c), residual[:, q]).then_inc(out_stored[q], 16)

            peeled(sp, half, work)
            for q in range(2):
                sp.wait_ge(out_stored[q], half * 16)
            shared.all_stored(sp)

        @block.gpsimd
        def _(pool):
            def fetch(c, q, nth, first_):
                tile = c * NT
                now = dest[:, tile:tile + NT, :] if isinstance(c, int) else dest[:, bass.ds(tile, NT), :]
                if not first_:
                    pool.wait_ge(consts, 1)
                    pool.wait_ge(summed, c - 1)
                pool.tensor_copy(dest_now[:, q], now).then_inc(numbers_ready[q], 1)
                pool.wait_ge(consts, 1)
                pool.wait_ge(numbers_ready[q], nth)
                for i in range(NT):
                    for k in range(TOP_K):
                        pool.indirect_dma_start(
                            from_experts[:, q, i, k, :], None, ys[:, :],
                            bass.IndirectOffsetOnAxis(ap=dest_now[:, q, i, k:k + 1], axis=0)).then_inc(gathered[q], 16)

            def finish(c, q):
                pool.wait_ge(mv_ready, c + 1)
                pool.tensor_tensor(vare[:], mv[:, :, 1], eps_t[:], ALU.add).then_inc(vare_ready, 1)
                pool.wait_ge(vare_ready, c + 1)
                pool.tensor_tensor(rstd[:], vare[:], mhalf_t[:], ALU.pow).then_inc(rstd_ready, 1)
                pool.wait_ge(normed, c + 1)
                pool.tensor_tensor(residual[:, q], residual[:, q], from_shared[:, q], ALU.add).then_inc(out_ready, 1)

            pool.memset(eps_t[:], EPS)
            pool.memset(mhalf_t[:], -0.5).then_inc(consts, 1)
            pool.wait_ge(consts, 1)
            for q in range(2):
                fetch(q, q, 1, True)
            with pool.Fori(2, half + 1) as nth:
                for c, q in blocks_of(nth - 2):
                    finish(c, q)
                    fetch(c + 2, q, nth, False)
            for c, q in blocks_of(half - 1):
                finish(c, q)

        @block.tensor
        def _(pe):
            shared.turn(pe, 0)
            peeled(pe, half, lambda j, first_, last: shared.tensor(pe, j, last))

        @block.scalar
        def _(act):
            shared.split_x_high(act, 0)
            peeled(act, half, lambda j, first_, last: shared.scalar(act, j, last))

        @block.vector
        def _(dve):
            def combine(c, q, j, first_):
                tile = c * NT
                now = gates[:, tile:tile + NT, :] if isinstance(c, int) else gates[:, bass.ds(tile, NT), :]
                dve.tensor_copy(gate_now[:, q], now).then_inc(gates_ready, 1)
                dve.wait_ge(gates_ready, c + 1)
                dve.wait_ge(loaded[q], (j + 1) * 32)
                dve.wait_ge(gathered[q], (j + 1) * 16 * NT * TOP_K)
                for k in range(TOP_K):
                    for i in range(NT):
                        ad = dve.scalar_tensor_tensor(from_shared[:, q, i, :], from_experts[:, q, i, k, :],
                                                      gate_now[:, q, i, k:k + 1], from_shared[:, q, i, :],
                                                      ALU.mult, ALU.add)
                    if k == 0:
                        ad.then_inc(added, 1)
                        dve.wait_ge(added, c + 1)
                ad.then_inc(summed, 1)
                dve.wait_ge(summed, c + 1)
                for i in range(NT):
                    st = dve.bn_stats(stats[:, i, :], from_shared[:, q, i, :])
                st.then_inc(stat_ready, 1)
                dve.wait_ge(gates_ready, 1)
                dve.wait_ge(stat_ready, c + 1)
                for i in range(NT):
                    ag = dve.bn_aggr(mv[:, i, :], stats[:, i, :])
                ag.then_inc(mv_ready, 1)
                dve.wait_ge(rstd_ready, c + 1)
                for i in range(NT):
                    nm = dve.tensor_scalar(from_shared[:, q, i, :], from_shared[:, q, i, :], mv[:, i, 0:1],
                                           rstd[:, i:i + 1], ALU.subtract, ALU.mult)
                nm.then_inc(normed, 1)

            def work(j, first_, last):
                shared.vector(dve, j, last)
                for c, q in blocks_of(j):
                    combine(c, q, j, first_)

            shared.split_x_low(dve, 0)
            peeled(dve, half, work)


def model(nc, x, wq, wk, wv, wo, w12T, w3T, sw1T, sw2T, sw3T, router_wT, expert_bias, rope_tables, masks, lanes, out):
    def dram(name, shape):
        return nc.dram_tensor(name, shape, F32, kind="Internal").ap()

    x1, xn2, shared_out = dram("x1", (B, T, C)), dram("xn2", (B, T, C)), dram("shared_out", (B, T, C))
    xs, ys = dram("expert_rows", (TILES * P, C)), dram("expert_results", (TILES * P, C))

    with ExitStack() as ctx:
        logits = ctx.enter_context(nc.sbuf_tensor("logits", [P, TOKEN_TILES, NE], F32))
        attention_phase(nc, x, wq, wk, wv, wo, router_wT, rope_tables, masks, x1, xn2, xs, logits)

        def sb(name, shape, dt=F32):
            return ctx.enter_context(nc.sbuf_tensor(name, shape, dt))

        w1_s, w2_s = (sb(n, [P, 2, KC, HID], F32R) for n in ("shared_w1_split", "shared_w2_split"))
        w3_s = sb("shared_w3_split", [P, 2, HID // P, C], F32R)
        ident = sb("ident", [P, P])
        dest = sb("dest", [P, TOKEN_TILES, TOP_K], mybir.dt.int32)
        gates = sb("gates", [P, TOKEN_TILES, TOP_K])
        experts = ctx.enter_context(ExitStack())
        w12_s = experts.enter_context(nc.sbuf_tensor("w12_split", [P, NE, 2, KC, 2 * HE], F32R))
        we3_s = experts.enter_context(nc.sbuf_tensor("w3_split", [P, NE, 2, KH, C], F32R))
        tile_expert = experts.enter_context(nc.sbuf_tensor("tile_expert", [1, TILES], mybir.dt.int32))

        with nc.semaphore("ident_loaded") as ident_loaded, nc.Block() as block:
            @block.sync
            def _(sp):
                sp.dma_start(ident[:], masks[0]).then_inc(ident_loaded, 16)
                sp.wait_ge(ident_loaded, 16)

        def by_rows(src, split, cols):
            return src.rearrange("(k p) n -> p k n", p=P), split, lambda a: a.rearrange("p (k n) -> p k n", n=cols)

        shared_w = []
        for w, split in ((sw1T, w1_s), (sw2T, w2_s)):
            for n in range(0, HID, 512):
                shared_w.append(by_rows(w[:, n:n + 512], lambda h, s=split, n=n: s[:, h, :, n:n + 512], 512))
        for m in range(0, HID // P, 4):
            shared_w.append(by_rows(sw3T[m * P:(m + 4) * P, :], lambda h, m=m: w3_s[:, h, m:m + 4, :], C))
        expert_w = []
        for e in range(NE):
            expert_w.append(by_rows(w12T[e], lambda h, e=e: w12_s[:, e, h], 2 * HE))
        for e in range(0, NE):
            src, split, shape = by_rows(w3T[e], lambda h, e=e: we3_s[:, e, h], C)
            expert_w.append((src, split, lambda a: a[:, 0:KH * C].rearrange("p (k n) -> p k n", n=C)))

        routing_phase(nc, xn2, xs, logits, expert_bias, lanes, masks, shared_w, expert_w, shared_out,
                      w1_s, w2_s, w3_s, w12_s, we3_s, ident[:], dest, gates, tile_expert)
        experts_phase(nc, xs, ys, w12_s, we3_s, ident[:], tile_expert)
        experts.close()
        combine_phase(nc, xn2, x1, ys, shared_out, w1_s, w2_s, w3_s, ident[:], dest, gates, out)


def rope_constants():
    inv_freq = np.float32(1) / np.float32(THETA) ** (np.arange(0, D, 2, dtype=np.float32) / np.float32(D))
    angle = (inv_freq[:, None] * np.arange(T, dtype=np.float32)[None, :]).astype(np.float64)
    cos = np.concatenate([np.cos(angle)] * 2)
    sin = np.concatenate([-np.sin(angle), np.sin(angle)])
    scale = 1 / np.sqrt(D)
    return np.stack([cos, sin, cos * scale, sin * scale]).astype(np.float32)


def mask_constants():
    row, col = np.indices((P, P))
    return np.stack([row == col, np.where(col > row, MASKED, 0), col > row]).astype(np.float32)


def lane_constants():
    return np.concatenate([np.tile(NE - np.arange(NE), P), np.arange(TILES)]).astype(np.float32)


_INS = ['L0_attn_hidden_states', 'L0_attn_Wq', 'L0_attn_Wk', 'L0_attn_Wv', 'L0_attn_Wo']
_TURNED = ['L0_ffn_w12', 'L0_ffn_w3', 'L0_ffn_shared_w1', 'L0_ffn_shared_w2', 'L0_ffn_shared_w3', 'L0_ffn_router_w']


def kernel(**inputs):
    import numpy as _np
    import concourse.bacc as _bacc
    from concourse import mybir as _mybir
    from concourse.bass_utils import run_bass_kernel_spmd as _run

    nc = _bacc.Bacc("TRN2", target_bir_lowering=False, num_devices=1)
    arrays, args = {}, []

    def given(name, a):
        arrays[f"in_{name}_dram"] = a
        args.append(nc.dram_tensor(f"in_{name}_dram", a.shape, _mybir.dt.from_np(a.dtype), kind="ExternalInput").ap())

    for name in _INS:
        given(name, _np.ascontiguousarray(inputs[name]))
    for name in _TURNED:
        given(name, _np.ascontiguousarray(_np.swapaxes(inputs[name], -1, -2)))
    given("L0_ffn_expert_bias", _np.ascontiguousarray(inputs["L0_ffn_expert_bias"]))
    given("rope_tables", rope_constants())
    given("masks", mask_constants())
    given("lanes", lane_constants())
    args.append(nc.dram_tensor("out_0_dram", (B, T, C), _mybir.dt.float32, kind="ExternalOutput").ap())
    model(nc, *args)
    r = _run(nc, [arrays], core_ids=[0])
    return r.results[0]["out_0_dram"]
```

```python
from contextlib import ExitStack

import numpy as np

import concourse.bass as bass
from concourse import mybir

F32 = mybir.dt.float32
F32R = mybir.dt.float32r
BF16 = mybir.dt.bfloat16
ALU = mybir.AluOpType
ACT = mybir.ActivationFunctionType
AX_X = mybir.AxisListType.X

P = 128
B, T, C = 16, 512, 256
NH, NKV, D = 8, 4, 128
KC = C // P
NT = T // P
NP = NH // 2
NE = 8
TOP_K = 2
HID = 1024
HE = 256
KH = HE // P
BLOCKS = B
TOKEN_TILES = B * NT
TILES = TOP_K * TOKEN_TILES + NE
EPS = 1e-5
THETA = 10000.0
MASKED = -3.0e38
TAKEN = -1.0e30

HI, LO = 0, 1
PASSES = ((HI, HI), (HI, LO), (LO, HI))

UNITS = (
    ((0, 3, 0),),
    ((1, 3, 0),),
    ((0, 2, 0), (0, 0, 384)),
    ((1, 2, 0), (1, 0, 384)),
    ((0, 1, 0), (1, 1, 256)),
)
NU = len(UNITS)

RING_START = 5
RING_PER_BATCH = 22
RING_ROPE = (0, 7, 10, 15)
RING_V = 3
RING_XT = 13
RING_ROUTER = 18
RING_ROUTER_LAST = 13
RING_ROUTER_END = 17


def wait_if_any(engine, semaphore, count):
    if not isinstance(count, int) or count > 0:
        engine.wait_ge(semaphore, count)


def rows_of(rows, b):
    return rows[b] if isinstance(b, int) else rows[bass.ds(b, 1)].rearrange("b p i c -> (b p) i c")


def attention_phase(nc, x, wq, wk, wv, wo, router_wT, rope_tables, masks, x1, xn2, xs, logits):
    with ExitStack() as ctx:
        def sb(name, shape, dt=F32):
            return ctx.enter_context(nc.sbuf_tensor(name, shape, dt))

        def ps(name):
            return ctx.enter_context(nc.psum_tensor(name, [P, T], F32))

        def sem(name):
            return ctx.enter_context(nc.semaphore(name))

        wq_s = sb("wq_split", [P, 2, KC, NH * D], F32R)
        wk_s = sb("wk_split", [P, 2, KC, NKV * D], F32R)
        wv_s = sb("wv_split", [P, 2, KC, NKV * D], F32R)
        wo_s = sb("wo_split", [P, 2, NH, C], F32R)
        wq_in = sb("wq_in", [P, KC, NH * D])
        wkv_in = sb("wkv_in", [P, 2, KC, NKV * D])
        tables = sb("tables", [P, 4, T])
        mask_in = sb("mask_in", [P, 2, P])
        ident_bf = sb("ident_bf", [P, P], BF16)
        causal_bf = sb("causal_bf", [P, P], BF16)
        eps_t = sb("eps_t", [P, NT])
        mhalf_t = sb("mhalf_t", [P, NT])
        ident = mask_in[:, 0, :]

        x_in = sb("x_in", [P, NT, C])
        x_res = sb("x_res", [P, NT, C])
        xn = sb("xn", [P, NT, C])
        yn = sb("yn", [P, NT, C])
        xn2_sb = wkv_in[:, 0].rearrange("p k n -> p (k n)").rearrange("p (i c) -> p i c", c=C)
        xn2T = wq_in[:, :, 0:T]
        router_w = sb("router_w", [P, KC, NE])
        filler = sb("filler", [P, C])
        x2_stats = sb("x2_stats", [P, NT, 6])
        x2_mv = sb("x2_mv", [P, NT, 2])
        x2_rstd = sb("x2_rstd", [P, NT])
        x2_vare = sb("x2_vare", [P, NT])
        xnT = sb("xnT", [P, 2, KC, T], F32R)
        stats = sb("stats", [P, NT, 6])
        mv = sb("mv", [P, NT, 2])
        rstd = sb("rstd", [P, NT])
        vare = sb("vare", [P, NT])
        y_stats = sb("y_stats", [P, NT, 6])
        y_mv = sb("y_mv", [P, NT, 2])
        y_rstd = sb("y_rstd", [P, NT])
        y_vare = sb("y_vare", [P, NT])

        rope_c = sb("rope_c", [P, 2, T])
        rope_s = sb("rope_s", [P, 2, T])
        roped = sb("roped", [P, 2, T])
        kq = sb("kq", [P, 2, 3, 2, T], F32R)
        v_s = sb("v_split", [P, 2, NT, NKV * D], F32R)
        probs = sb("probs", [P, NU, T])
        wo_in = probs[:, 0:NH * C // T, :].rearrange("p u (h c) -> p (u h) c", c=C)
        neg_max = sb("neg_max", [P, NU, 2])
        row_sum = sb("row_sum", [P, NU, 2])
        row_inv = sb("row_inv", [P, NU, 2])
        pT = sb("pT", [P, 2, 2, NT, T], F32R)
        oT = sb("oT", [P, 2, 2, T], F32R)

        ring = [ps("ring0"), ps("ring1")]
        s_ps = [ps("s_ps0"), ps("s_ps1")]
        t_ps = ps("t_ps")
        o_ps = ps("o_ps")
        y_ps = [ps("y_ps0"), ps("y_ps1")]

        w_loaded = [sem(f"w_loaded{n}") for n in range(4)]
        masks_loaded = sem("masks_loaded")
        consts_loaded = sem("consts_loaded")
        x_loaded = sem("x_loaded")
        res_loaded = sem("res_loaded")
        x1_stored = sem("x1_stored")
        w_hi = sem("w_hi")
        w_lo = sem("w_lo")
        masks_ready = sem("masks_ready")
        pool_consts = sem("pool_consts")
        ln_stats = sem("ln_stats")
        ln_mv = sem("ln_mv")
        ln_vare = sem("ln_vare")
        ln_rstd = sem("ln_rstd")
        xn_ready = sem("xn_ready")
        y_st = sem("y_st")
        y_mvs = sem("y_mvs")
        y_ve = sem("y_ve")
        y_rs = sem("y_rs")
        yn_ready = sem("yn_ready")
        x1_ready = sem("x1_ready")
        filler_ready = sem("filler_ready")
        xs_filled = sem("xs_filled")
        xn2_stored = sem("xn2_stored")
        x2_st = sem("x2_st")
        x2_mvs = sem("x2_mvs")
        x2_ve = sem("x2_ve")
        x2_rs = sem("x2_rs")
        xn2_ready = sem("xn2_ready")
        ring_full = sem("ring_full")
        ring_free = sem("ring_free")
        xT_hi = sem("xT_hi")
        v_hi = sem("v_hi")
        rope_sum = sem("rope_sum")
        kq_hi = sem("kq_hi")
        kq_lo = sem("kq_lo")
        scores_ready = sem("scores_ready")
        max_ready = sem("max_ready")
        exp_ready = sem("exp_ready")
        inv_ready = sem("inv_ready")
        probs_ready = sem("probs_ready")
        pT_full = sem("pT_full")
        pT_hi = sem("pT_hi")
        pT_lo = sem("pT_lo")
        o_full = sem("o_full")
        oT_hi = sem("oT_hi")
        oT_lo = sem("oT_lo")
        y_full = sem("y_full")

        x_rows = x.rearrange("b (i p) c -> b p i c", p=P)
        x1_rows = x1.rearrange("b (i p) c -> b p i c", p=P)
        xn2_rows = xn2.rearrange("b (i p) c -> b p i c", p=P)

        def batches(engine, slot_work):
            slot_work(0, True, False)
            with engine.Fori(1, B - 1) as b:
                slot_work(b, False, False)
            slot_work(B - 1, False, True)

        def ring_base(b):
            router_units = RING_PER_BATCH - RING_ROUTER
            return RING_START if isinstance(b, int) and b == 0 else b * RING_PER_BATCH + RING_START - router_units

        def ring_unit(b, offset):
            return ring_base(b) + offset, ring[(RING_START + offset) % 2]

        block = ctx.enter_context(nc.Block())

        @block.sync
        def _(sp):
            sp.dma_start(x_in[:], x_rows[0]).then_inc(x_loaded, 16)
            sp.dma_start(mask_in[:], masks[0:2].rearrange("m p c -> p m c")).then_inc(masks_loaded, 16)
            sp.dma_start(wkv_in[:, 0], wk.rearrange("(k p) n -> p k n", p=P)).then_inc(w_loaded[0], 16)
            sp.dma_start(wq_in[:], wq.rearrange("(k p) n -> p k n", p=P)).then_inc(w_loaded[1], 16)
            sp.dma_start(tables[:], rope_tables.rearrange("m p t -> p m t")).then_inc(consts_loaded, 16)
            sp.dma_start(wkv_in[:, 1], wv.rearrange("(k p) n -> p k n", p=P)).then_inc(w_loaded[2], 16)
            sp.dma_start(wo_in[:], wo.rearrange("(h p) n -> p h n", p=P)).then_inc(w_loaded[3], 16)
            sp.dma_start(router_w[:], router_wT.rearrange("(k p) e -> p k e", p=P)).then_inc(consts_loaded, 16)

            def work(b, first, last):
                if not last:
                    sp.wait_ge(xn_ready, b + 1)
                    sp.dma_start(x_in[:], rows_of(x_rows, b + 1)).then_inc(x_loaded, 16)
                if not first:
                    sp.wait_ge(x1_ready, b)
                    sp.dma_start(rows_of(x1_rows, b - 1), yn[:]).then_inc(x1_stored, 16)
                sp.dma_start(x_res[:], rows_of(x_rows, b)).then_inc(res_loaded, 16)
                if first:
                    sp.wait_ge(filler_ready, 1)
                    for n in range(TILES):
                        sp.dma_start(xs[n * P:(n + 1) * P, :], filler[:]).then_inc(xs_filled, 16)
                if not first:
                    sp.wait_ge(xn2_ready, b)
                    sp.dma_start(rows_of(xn2_rows, b - 1), xn2_sb).then_inc(xn2_stored, 16)

            batches(sp, work)
            sp.wait_ge(x1_ready, B)
            sp.dma_start(x1_rows[B - 1], yn[:]).then_inc(x1_stored, 16)
            sp.wait_ge(xn2_ready, B)
            sp.dma_start(xn2_rows[B - 1], xn2_sb).then_inc(xn2_stored, 16)
            sp.wait_ge(x1_stored, 16 * B)
            sp.wait_ge(xn2_stored, 16 * B)
            sp.wait_ge(xs_filled, 16 * TILES)

        @block.tensor
        def _(pe):
            def transpose_xn(b_next, unit0, bank_of):
                pe.wait_ge(xn_ready, b_next + 1)
                for k in range(KC):
                    wait_if_any(pe, ring_free, unit0 + k - 1)
                    for i in range(NT):
                        mm = pe.transpose(bank_of(k)[:, i * P:(i + 1) * P], xn[:, i, k * P:(k + 1) * P], ident)
                    mm.then_inc(ring_full, 1)

            def project_pair(j, p, unit, bank):
                wait_if_any(pe, ring_free, unit - 1)
                w, head = (wk_s, p) if j == 0 else (wq_s, 2 * p + j - 1)
                n = 0
                for a, c in PASSES:
                    for k in range(KC):
                        mm = pe.matmul(bank[:], w[:, a, k, head * D:(head + 1) * D], xnT[:, c, k, :],
                                       start=(n == 0), stop=(n == 3 * KC - 1))
                        n += 1
                mm.then_inc(ring_full, 1)

            def project_v(i, unit, bank):
                pe.wait_ge(ring_free, unit - 1)
                n = 0
                for a, c in PASSES:
                    for k in range(KC):
                        mm = pe.matmul(bank[:], xnT[:, a, k, i * P:(i + 1) * P], wv_s[:, c, k, :],
                                       start=(n == 0), stop=(n == 3 * KC - 1))
                        n += 1
                mm.then_inc(ring_full, 1)

            def scores(b, p, u):
                g = b * (NP * NU) + p * NU + u
                pair = b * NP + p
                pe.wait_ge(kq_lo, pair * 3 + (3 if any(h for h, _, _ in UNITS[u]) else 2))
                wait_if_any(pe, exp_ready, g - 1)
                bank = s_ps[(p * NU + u) % 2]
                for h, i, c0 in UNITS[u]:
                    keys = (i + 1) * P
                    for n, (a, c) in enumerate(PASSES):
                        pe.matmul(bank[:, c0:c0 + keys], kq[:, p % 2, 1 + h, a, i * P:(i + 1) * P],
                                  kq[:, p % 2, 0, c, 0:keys], start=(n == 0), stop=False)
                    mm = pe.matmul(bank[:, c0 + i * P:c0 + keys], ident_bf[:], causal_bf[:], start=False, stop=True)
                mm.then_inc(scores_ready, 1)

            def transposes(b, p, u):
                g = b * (NP * NU) + p * NU + u
                pe.wait_ge(probs_ready, g + 1)
                wait_if_any(pe, pT_lo, g)
                for h, i, c0 in UNITS[u]:
                    for j in range(i + 1):
                        c = c0 + j * P
                        mm = pe.transpose(t_ps[:, c:c + P], probs[:, u, c:c + P], ident)
                mm.then_inc(pT_full, 1)

            def values(b, p, h):
                n = b * NH + 2 * p + h
                pair = b * NP + p
                pe.wait_ge(pT_lo, (pair + 1) * NU)
                if p == 0:
                    pe.wait_ge(ring_free, ring_base(b) + RING_V + NT)
                wait_if_any(pe, oT_lo, n)
                for j in range(NT):
                    for m, (a, c) in enumerate(PASSES):
                        mm = pe.matmul(o_ps[:, j * P:T], v_s[:, a, j, p * D:(p + 1) * D], pT[:, c, h, j, j * P:T],
                                       start=(j == 0 and m == 0), stop=(j == NT - 1 and m == 2))
                mm.then_inc(o_full, 1)

            def out_projection(b, p, h):
                n = b * NH + 2 * p + h
                pe.wait_ge(oT_lo, n + 1)
                if p == 0 and h == 0:
                    wait_if_any(pe, yn_ready, b)
                for i in range(NT):
                    for m, (a, c) in enumerate(PASSES):
                        mm = pe.matmul(y_ps[i // 2][:, (i % 2) * C:(i % 2 + 1) * C],
                                       oT[:, a, h, i * P:(i + 1) * P], wo_s[:, c, 2 * p + h, :],
                                       start=(p == 0 and h == 0 and m == 0 and i % 2 == 0),
                                       stop=(p == NP - 1 and h == 1 and m == 2), skip_group_check=True)
                mm.then_inc(y_full, 1)

            def transpose_xn2(b, unit0, bank0):
                pe.wait_ge(xn2_ready, b + 1)
                for k in range(KC):
                    pe.wait_ge(ring_free, unit0 + k - 1)
                    for i in range(NT):
                        mm = pe.transpose(ring[(bank0 + k) % 2][:, i * P:(i + 1) * P], xn2_sb[:, i, k * P:(k + 1) * P],
                                          ident)
                    mm.then_inc(ring_full, 1)

            def route(unit0, bank0):
                for n in range(2):
                    pe.wait_ge(ring_free, unit0 + 2)
                    for i in range(2 * n, 2 * n + 2):
                        for k in range(KC):
                            mm = pe.matmul(ring[(bank0 + n) % 2][:, (i % 2) * NE:(i % 2 + 1) * NE],
                                           xn2T[:, k, i * P:(i + 1) * P], router_w[:, k, :],
                                           start=(k == 0), stop=(k == KC - 1))
                    mm.then_inc(ring_full, 1)

            def work(b, first, last):
                router = RING_ROUTER_LAST if last else RING_ROUTER
                for p in range(NP):
                    more = not (last and p == NP - 1)
                    before = not (first and p == 0)
                    pb, pp = (b, p - 1) if p else (b - 1, NP - 1)

                    def project(j):
                        if more:
                            if j == 0 and p == NP - 1:
                                pe.wait_ge(ring_free, ring_base(b) + RING_XT + KC)
                            project_pair(j, (p + 1) % NP, *ring_unit(b, RING_ROPE[p] + j))

                    def project_values(i):
                        if p == 0:
                            project_v(i, *ring_unit(b, RING_V + i))

                    scores(b, p, 0)
                    if before:
                        transposes(pb, pp, 3)
                    project(0)

                    scores(b, p, 1)
                    if before:
                        transposes(pb, pp, 4)
                    project(1)
                    if before:
                        values(pb, pp, 0)

                    scores(b, p, 2)
                    transposes(b, p, 0)
                    if before:
                        values(pb, pp, 1)

                    scores(b, p, 3)
                    project(2)
                    transposes(b, p, 1)
                    project_values(0)
                    if before:
                        out_projection(pb, pp, 0)
                    if p == 3 and not first:
                        out_projection(pb, pp, 1)
                        transpose_xn2(b - 1, ring_base(b) + router, RING_START + router)
                    project_values(1)

                    scores(b, p, 4)
                    transposes(b, p, 2)
                    project_values(2)
                    if p == 2 and not last:
                        transpose_xn(b + 1, ring_unit(b, RING_XT)[0], lambda k: ring_unit(0, RING_XT + k)[1])
                    if before and (p < 3 or first):
                        out_projection(pb, pp, 1)
                    project_values(3)
                    if p == 3 and not first:
                        route(ring_base(b) + router, RING_START + router)

            pe.wait_ge(masks_loaded, 16)
            transpose_xn(0, 0, lambda k: ring[k % 2])
            pe.wait_ge(masks_ready, 2)
            pe.wait_ge(w_lo, 2)
            pe.wait_ge(ring_free, KC)
            for j in range(3):
                project_pair(j, 0, KC + j, ring[(KC + j) % 2])
            pe.wait_ge(w_lo, 4)
            pe.wait_ge(consts_loaded, 32)
            batches(pe, work)
            for u in (3, 4):
                transposes(B - 1, NP - 1, u)
            for h in range(2):
                values(B - 1, NP - 1, h)
            for h in range(2):
                out_projection(B - 1, NP - 1, h)
            end = ring_base(B - 1) + RING_ROUTER_END
            transpose_xn2(B - 1, end, RING_START + RING_ROUTER_END)
            route(end, RING_START + RING_ROUTER_END)

        @block.scalar
        def _(act):
            def high_part(out, in_):
                return act.activation(out, in_, ACT.Copy)

            def exponentials(b, p, u):
                g = b * (NP * NU) + p * NU + u
                act.wait_ge(max_ready, g + 1)
                for n, (h, i, c0) in enumerate(UNITS[u]):
                    keys = (i + 1) * P
                    ex = act.activation(probs[:, u, c0:c0 + keys], s_ps[(p * NU + u) % 2][:, c0:c0 + keys], ACT.Exp,
                                        bias=neg_max[:, u, n:n + 1], accum_out=row_sum[:, u, n:n + 1])
                ex.then_inc(exp_ready, 1)

            def normalise(b, p, u):
                g = b * (NP * NU) + p * NU + u
                act.wait_ge(inv_ready, g + 1)
                for n, (h, i, c0) in enumerate(UNITS[u]):
                    keys = (i + 1) * P
                    nm = act.activation(probs[:, u, c0:c0 + keys], probs[:, u, c0:c0 + keys], ACT.Copy,
                                        scale=row_inv[:, u, n:n + 1])
                nm.then_inc(probs_ready, 1)

            def pT_high(b, p, u):
                g = b * (NP * NU) + p * NU + u
                act.wait_ge(pT_full, g + 1)
                if u == 0:
                    wait_if_any(act, o_full, (b * NP + p) * 2)
                for h, i, c0 in UNITS[u]:
                    hi = high_part(pT[:, HI, h, 0:i + 1, i * P:(i + 1) * P],
                                   t_ps[:, c0:c0 + (i + 1) * P].rearrange("p (j t) -> p j t", t=P))
                hi.then_inc(pT_hi, 1)

            def oT_high(b, p, h):
                n = b * NH + 2 * p + h
                act.wait_ge(o_full, n + 1)
                wait_if_any(act, y_full, n - 1)
                high_part(oT[:, HI, h, :], o_ps[:]).then_inc(oT_hi, 1)

            def kq_high(pair, parity, j):
                act.wait_ge(rope_sum, pair * 3 + j + 1)
                high_part(kq[:, parity, j, HI, :], roped[:, (parity * 3 + j) % 2, :]).then_inc(kq_hi, 1)

            def v_high(b, i):
                act.wait_ge(ring_full, ring_base(b) + RING_V + i + 1)
                if i == 0:
                    wait_if_any(act, o_full, b * NH)
                high_part(v_s[:, HI, i, :], ring[(RING_START + RING_V + i) % 2][:]).then_inc(v_hi, 1)

            def xT_high(b_next, unit, k, bank):
                act.wait_ge(ring_full, unit + 1)
                high_part(xnT[:, HI, k, :], bank[:]).then_inc(xT_hi, 1)

            def work(b, first, last):
                for p in range(NP):
                    more = not (last and p == NP - 1)
                    before = not (first and p == 0)
                    pb, pp = (b, p - 1) if p else (b - 1, NP - 1)

                    def kq_next(j):
                        if more:
                            kq_high(b * NP + p + 1, (p + 1) % 2, j)

                    def v_next(i):
                        if p == 0:
                            v_high(b, i)

                    if before:
                        pT_high(pb, pp, 3)
                    exponentials(b, p, 0)
                    if before:
                        pT_high(pb, pp, 4)
                    exponentials(b, p, 1)
                    normalise(b, p, 0)
                    if before:
                        oT_high(pb, pp, 0)
                    kq_next(0)
                    normalise(b, p, 1)
                    exponentials(b, p, 2)
                    pT_high(b, p, 0)
                    if before:
                        oT_high(pb, pp, 1)
                    kq_next(1)
                    normalise(b, p, 2)
                    pT_high(b, p, 1)
                    exponentials(b, p, 3)
                    normalise(b, p, 3)
                    v_next(0)
                    v_next(1)
                    pT_high(b, p, 2)
                    exponentials(b, p, 4)
                    v_next(2)
                    if p == 2 and not last:
                        for k in range(KC):
                            xT_high(b + 1, ring_unit(b, RING_XT + k)[0], k, ring[(RING_START + RING_XT + k) % 2])
                    kq_next(2)
                    v_next(3)
                    normalise(b, p, 4)

            for k in range(KC):
                xT_high(0, k, k, ring[k % 2])
            act.wait_ge(w_loaded[0], 16)
            high_part(wk_s[:, HI], wkv_in[:, 0]).then_inc(w_hi, 1)
            act.wait_ge(w_loaded[1], 16)
            high_part(wq_s[:, HI], wq_in[:]).then_inc(w_hi, 1)
            act.wait_ge(w_loaded[2], 16)
            high_part(wv_s[:, HI], wkv_in[:, 1]).then_inc(w_hi, 1)
            act.wait_ge(w_loaded[3], 16)
            high_part(wo_s[:, HI], wo_in[:]).then_inc(w_hi, 1)
            for j in range(3):
                kq_high(0, 0, j)
            batches(act, work)
            for u in (3, 4):
                pT_high(B - 1, NP - 1, u)
            for h in range(2):
                oT_high(B - 1, NP - 1, h)

        @block.vector
        def _(dve):
            def low_part(out, in_, high):
                return dve.tensor_tensor(out, in_, high.bitcast(F32), ALU.subtract)

            def row_max(b, p, u):
                g = b * (NP * NU) + p * NU + u
                dve.wait_ge(scores_ready, g + 1)
                for n, (h, i, c0) in enumerate(UNITS[u]):
                    mx = dve.tensor_reduce(neg_max[:, u, n:n + 1], s_ps[(p * NU + u) % 2][:, c0:c0 + (i + 1) * P],
                                           AX_X, ALU.max, negate=True)
                mx.then_inc(max_ready, 1)

            def inverse(b, p, u):
                g = b * (NP * NU) + p * NU + u
                n = len(UNITS[u])
                dve.wait_ge(exp_ready, g + 1)
                dve.reciprocal(row_inv[:, u, 0:n], row_sum[:, u, 0:n]).then_inc(inv_ready, 1)

            def pT_low(b, p, u):
                g = b * (NP * NU) + p * NU + u
                dve.wait_ge(pT_hi, g + 1)
                for h, i, c0 in UNITS[u]:
                    cols = slice(i * P, (i + 1) * P)
                    lo = low_part(pT[:, LO, h, 0:i + 1, cols],
                                  t_ps[:, c0:c0 + (i + 1) * P].rearrange("p (j t) -> p j t", t=P),
                                  pT[:, HI, h, 0:i + 1, cols])
                lo.then_inc(pT_lo, 1)

            def oT_low(b, p, h):
                n = b * NH + 2 * p + h
                dve.wait_ge(oT_hi, n + 1)
                low_part(oT[:, LO, h, :], o_ps[:], oT[:, HI, h, :]).then_inc(oT_lo, 1)

            def rotate_cos(pair, j, parity, unit, bank):
                n = pair * 3 + j
                r = (parity * 3 + j) % 2
                t = 0 if j == 0 else 2
                dve.wait_ge(ring_full, unit + 1)
                wait_if_any(dve, rope_sum, n - 1)
                dve.tensor_tensor(rope_c[:, r, :], bank[:], tables[:, t, :], ALU.mult)

            def rotate_sin(pair, j, parity, unit, bank):
                r = (parity * 3 + j) % 2
                t = 0 if j == 0 else 2
                half = D // 2
                dve.tensor_tensor(rope_s[0:half, r, :], bank[half:D], tables[0:half, t + 1, :], ALU.mult)
                dve.tensor_tensor(rope_s[half:D, r, :], bank[0:half], tables[half:D, t + 1, :],
                                  ALU.mult).then_inc(ring_free, 1)

            def rotate(*which):
                rotate_cos(*which)
                rotate_sin(*which)

            def v_low(b, i):
                dve.wait_ge(v_hi, b * NT + i + 1)
                low_part(v_s[:, LO, i, :], ring[(RING_START + RING_V + i) % 2][:], v_s[:, HI, i, :]).then_inc(ring_free, 1)

            def xT_low(b_next, k, bank):
                dve.wait_ge(xT_hi, b_next * KC + k + 1)
                low_part(xnT[:, LO, k, :], bank[:], xnT[:, HI, k, :]).then_inc(ring_free, 1)

            def ln_statistics(b_next):
                dve.wait_ge(x_loaded, (b_next + 1) * 16)
                for i in range(NT):
                    st = dve.bn_stats(stats[:, i, :], x_in[:, i, :])
                st.then_inc(ln_stats, 1)
                dve.wait_ge(x_loaded, 16)
                dve.wait_ge(ln_stats, b_next + 1)
                for i in range(NT):
                    ag = dve.bn_aggr(mv[:, i, :], stats[:, i, :])
                ag.then_inc(ln_mv, 1)

            def ln_apply(b_next):
                dve.wait_ge(ln_rstd, b_next + 1)
                for i in range(NT):
                    ap = dve.tensor_scalar(xn[:, i, :], x_in[:, i, :], mv[:, i, 0:1], rstd[:, i:i + 1],
                                           ALU.subtract, ALU.mult)
                ap.then_inc(xn_ready, 1)

            def y_of(i):
                return y_ps[i // 2][:, (i % 2) * C:(i % 2 + 1) * C]

            def y_statistics(b):
                dve.wait_ge(y_full, (b + 1) * NH)
                for i in range(NT):
                    st = dve.bn_stats(y_stats[:, i, :], y_of(i))
                st.then_inc(y_st, 1)
                dve.wait_ge(x_loaded, 16)
                dve.wait_ge(y_st, b + 1)
                for i in range(NT):
                    ag = dve.bn_aggr(y_mv[:, i, :], y_stats[:, i, :])
                ag.then_inc(y_mvs, 1)

            def y_apply(b):
                dve.wait_ge(y_rs, b + 1)
                wait_if_any(dve, x1_stored, b * 16)
                for i in range(NT):
                    ap = dve.tensor_scalar(yn[:, i, :], y_of(i), y_mv[:, i, 0:1], y_rstd[:, i:i + 1],
                                           ALU.subtract, ALU.mult)
                ap.then_inc(yn_ready, 1)

            def x2_statistics(b):
                dve.wait_ge(x1_ready, b + 1)
                for i in range(NT):
                    st = dve.bn_stats(x2_stats[:, i, :], yn[:, i, :])
                st.then_inc(x2_st, 1)
                dve.wait_ge(x_loaded, 16)
                dve.wait_ge(x2_st, b + 1)
                for i in range(NT):
                    ag = dve.bn_aggr(x2_mv[:, i, :], x2_stats[:, i, :])
                ag.then_inc(x2_mvs, 1)

            def x2_apply(b):
                dve.wait_ge(x2_rs, b + 1)
                wait_if_any(dve, xn2_stored, b * 16)
                for i in range(NT):
                    ap = dve.tensor_scalar(xn2_sb[:, i, :], yn[:, i, :], x2_mv[:, i, 0:1], x2_rstd[:, i:i + 1],
                                           ALU.subtract, ALU.mult)
                ap.then_inc(xn2_ready, 1)

            def copy_xn2T(unit0, bank0):
                for k in range(KC):
                    dve.wait_ge(ring_full, unit0 + k + 1)
                    dve.tensor_copy(xn2T[:, k, :], ring[(bank0 + k) % 2][:]).then_inc(ring_free, 1)

            def keep_logits(b, unit0, bank0):
                for n in range(2):
                    dve.wait_ge(ring_full, unit0 + n + 3)
                    tile = b * NT + 2 * n
                    to = logits[:, tile:tile + 2, :] if isinstance(b, int) else logits[:, bass.ds(tile, 2), :]
                    dve.tensor_scalar(to, ring[(bank0 + n) % 2][:, 0:2 * NE].rearrange("p (i e) -> p i e", e=NE),
                                      1.0, None, ALU.mult).then_inc(ring_free, 1)

            def work(b, first, last):
                router = RING_ROUTER_LAST if last else RING_ROUTER
                for p in range(NP):
                    more = not (last and p == NP - 1)
                    before = not (first and p == 0)
                    pb, pp = (b, p - 1) if p else (b - 1, NP - 1)

                    def rotate_next(j, part=rotate):
                        if more:
                            part(b * NP + p + 1, j, (p + 1) % 2, *ring_unit(b, RING_ROPE[p] + j))

                    def v_next(i):
                        if p == 0:
                            v_low(b, i)

                    row_max(b, p, 0)
                    if before:
                        pT_low(pb, pp, 3)
                    rotate_next(0, rotate_cos)
                    row_max(b, p, 1)
                    inverse(b, p, 0)
                    if before:
                        pT_low(pb, pp, 4)
                    if p == 1 and not first:
                        y_statistics(b - 1)
                    rotate_next(0, rotate_sin)
                    rotate_next(1, rotate_cos)
                    inverse(b, p, 1)
                    if before:
                        oT_low(pb, pp, 0)
                    row_max(b, p, 2)
                    rotate_next(1, rotate_sin)
                    if p == 1 and not first:
                        y_apply(b - 1)
                    if p == 0 and not last:
                        ln_statistics(b + 1)
                    if p == 2 and not first:
                        x2_statistics(b - 1)
                    if p == 3 and not first:
                        x2_apply(b - 1)
                    inverse(b, p, 2)
                    pT_low(b, p, 0)
                    if before:
                        oT_low(pb, pp, 1)
                    row_max(b, p, 3)
                    rotate_next(2, rotate_cos)
                    pT_low(b, p, 1)
                    rotate_next(2, rotate_sin)
                    inverse(b, p, 3)
                    v_next(0)
                    v_next(1)
                    if p == 3 and not first:
                        copy_xn2T(ring_base(b) + router, RING_START + router)
                    row_max(b, p, 4)
                    pT_low(b, p, 2)
                    v_next(2)
                    inverse(b, p, 4)
                    if p == 2 and not last:
                        for k in range(KC):
                            xT_low(b + 1, k, ring[(RING_START + RING_XT + k) % 2])
                    v_next(3)
                    if p == 1 and not last:
                        ln_apply(b + 1)
                    if p == 3 and not first:
                        keep_logits(b - 1, ring_base(b) + router, RING_START + router)

            ln_statistics(0)
            ln_apply(0)
            for k in range(KC):
                xT_low(0, k, ring[k % 2])
            dve.wait_ge(masks_loaded, 16)
            dve.tensor_copy(ident_bf[:], mask_in[:, 0, :]).then_inc(masks_ready, 1)
            dve.tensor_copy(causal_bf[:], mask_in[:, 1, :]).then_inc(masks_ready, 1)

            def weight_low(n, split, whole):
                dve.wait_ge(w_hi, n + 1)
                low_part(split[:, LO], whole, split[:, HI]).then_inc(w_lo, 1)

            weight_low(0, wk_s, wkv_in[:, 0])
            weight_low(1, wq_s, wq_in[:])
            dve.wait_ge(consts_loaded, 32)
            rotate(0, 0, 0, KC, ring[KC % 2])
            weight_low(2, wv_s, wkv_in[:, 1])
            rotate(0, 1, 0, KC + 1, ring[(KC + 1) % 2])
            weight_low(3, wo_s, wo_in[:])
            rotate(0, 2, 0, KC + 2, ring[(KC + 2) % 2])
            batches(dve, work)
            for u in (3, 4):
                pT_low(B - 1, NP - 1, u)
            for h in range(2):
                oT_low(B - 1, NP - 1, h)
            y_statistics(B - 1)
            y_apply(B - 1)
            x2_statistics(B - 1)
            x2_apply(B - 1)
            end = ring_base(B - 1) + RING_ROUTER_END
            copy_xn2T(end, RING_START + RING_ROUTER_END)
            keep_logits(B - 1, end, RING_START + RING_ROUTER_END)

        @block.gpsimd
        def _(pool):
            def inverse_std(count, mv_, vare_, rstd_, mv_ready, vare_ready, rstd_ready):
                pool.wait_ge(mv_ready, count)
                pool.tensor_tensor(vare_[:], mv_[:, :, 1], eps_t[:], ALU.add).then_inc(vare_ready, 1)
                pool.wait_ge(vare_ready, count)
                pool.tensor_tensor(rstd_[:], vare_[:], mhalf_t[:], ALU.pow).then_inc(rstd_ready, 1)

            def add_products(pair, j, parity, unit):
                n = pair * 3 + j
                r = (parity * 3 + j) % 2
                pool.wait_ge(ring_free, unit + 1)
                wait_if_any(pool, kq_lo, n - 1)
                pool.tensor_tensor(roped[:, r, :], rope_c[:, r, :], rope_s[:, r, :], ALU.add).then_inc(rope_sum, 1)

            def kq_low(pair, j, parity):
                r = (parity * 3 + j) % 2
                pool.wait_ge(kq_hi, pair * 3 + j + 1)
                pool.tensor_tensor(kq[:, parity, j, LO, :], roped[:, r, :], kq[:, parity, j, HI, :].bitcast(F32),
                                   ALU.subtract).then_inc(kq_lo, 1)

            def pair_work(pair, parity, unit0, heads=range(3)):
                for j in heads:
                    add_products(pair, j, parity, unit0 + j)
                    kq_low(pair, j, parity)

            def add_residual(b):
                pool.wait_ge(yn_ready, b + 1)
                pool.wait_ge(res_loaded, (b + 1) * 16)
                pool.tensor_tensor(yn[:], yn[:], x_res[:], ALU.add).then_inc(x1_ready, 1)

            def work(b, first, last):
                for p in range(NP):
                    def pair_next(heads):
                        if not (last and p == NP - 1):
                            pair_work(b * NP + p + 1, (p + 1) % 2, ring_unit(b, RING_ROPE[p])[0], heads)

                    if p == 1 and not first:
                        inverse_std(b, y_mv, y_vare, y_rstd, y_mvs, y_ve, y_rs)
                    pair_next(range(2))
                    if p == 0 and not last:
                        inverse_std(b + 2, mv, vare, rstd, ln_mv, ln_vare, ln_rstd)
                    if p == 2 and not first:
                        inverse_std(b, x2_mv, x2_vare, x2_rstd, x2_mvs, x2_ve, x2_rs)
                    pair_next(range(2, 3))
                    if p == 1 and not first:
                        add_residual(b - 1)

            pool.memset(filler[:], 0.0).then_inc(filler_ready, 1)
            pool.memset(eps_t[:], EPS)
            pool.memset(mhalf_t[:], -0.5).then_inc(pool_consts, 1)
            pool.wait_ge(pool_consts, 1)
            inverse_std(1, mv, vare, rstd, ln_mv, ln_vare, ln_rstd)
            pair_work(0, 0, KC)
            batches(pool, work)
            inverse_std(B, y_mv, y_vare, y_rstd, y_mvs, y_ve, y_rs)
            add_residual(B - 1)
            inverse_std(B, x2_mv, x2_vare, x2_rstd, x2_mvs, x2_ve, x2_rs)


def shared_ffn(nc, ctx, name, xn2, shared_out, w1_s, w2_s, w3_s, ident, first_block, blocks):
    units = HID // P

    def sb(what, shape, dt=F32):
        return ctx.enter_context(nc.sbuf_tensor(f"{name}_{what}", shape, dt))

    def ps(what):
        return ctx.enter_context(nc.psum_tensor(f"{name}_{what}", [P, T], F32))

    def sem(what):
        return ctx.enter_context(nc.semaphore(f"{name}_{what}"))

    x_in = sb("x_in", [P, NT, C])
    xT = sb("xT", [P, 2, KC, T], F32R)
    gate = sb("gate", [P, 2, T])
    hidden = sb("hidden", [P, 2, T])
    h_s = sb("h_split", [P, 2, 2, T], F32R)
    out = sb("out", [P, NT, C])
    h1_ps = [ps("h1_ps0"), ps("h1_ps1")]
    h2_ps = [ps("h2_ps0"), ps("h2_ps1")]
    x_ps = [ps("x_ps0"), ps("x_ps1")]
    y_ps = [ps("y_ps0"), ps("y_ps1")]
    x_loaded, x_turned, xT_hi, xT_lo = sem("x_loaded"), sem("x_turned"), sem("xT_hi"), sem("xT_lo")
    h1_full, h2_full, gate_ready, hidden_ready = sem("h1_full"), sem("h2_full"), sem("gate_ready"), sem("hidden_ready")
    h_hi, h_lo, y_full, out_ready, stored = sem("h_hi"), sem("h_lo"), sem("y_full"), sem("out_ready"), sem("stored")

    x_rows = xn2.rearrange("b (i p) c -> b p i c", p=P)
    out_rows = shared_out.rearrange("b (i p) c -> b p i c", p=P)

    class work:

        x_psum = x_ps
        output = out
        output_ready = out_ready

        def load(sp, j):
            wait_if_any(sp, x_turned, j * KC)
            sp.dma_start(x_in[:], rows_of(x_rows, first_block + j)).then_inc(x_loaded, 16)

        def store(sp, j):
            sp.wait_ge(out_ready, (j + 1) * 2)
            sp.dma_start(rows_of(out_rows, first_block + j), out[:]).then_inc(stored, 16)

        def turn(pe, j):
            pe.wait_ge(x_loaded, (j + 1) * 16)
            wait_if_any(pe, xT_lo, j * KC)
            for k in range(KC):
                for i in range(NT):
                    mm = pe.transpose(x_ps[k][:, i * P:(i + 1) * P], x_in[:, i, k * P:(k + 1) * P], ident)
                mm.then_inc(x_turned, 1)

        def tensor(pe, j, last, before_up=lambda m: None, before_down=lambda m: None):
            def up(m):
                before_up(m)
                if m == 0:
                    pe.wait_ge(xT_lo, (j + 1) * KC)
                wait_if_any(pe, hidden_ready, j * units + m - 1)
                for w, bank, full in ((w1_s, h1_ps[m % 2], h1_full), (w2_s, h2_ps[m % 2], h2_full)):
                    n = 0
                    for a, c in PASSES:
                        for k in range(KC):
                            mm = pe.matmul(bank[:], w[:, a, k, m * P:(m + 1) * P], xT[:, c, k, :],
                                           start=(n == 0), stop=(n == 3 * KC - 1))
                            n += 1
                    mm.then_inc(full, 1)

            def down(m):
                before_down(m)
                pe.wait_ge(h_lo, j * units + m + 1)
                if m == 0:
                    wait_if_any(pe, out_ready, j * 2)
                for i in range(NT):
                    for n, (a, c) in enumerate(PASSES):
                        mm = pe.matmul(y_ps[i // 2][:, (i % 2) * C:(i % 2 + 1) * C],
                                       h_s[:, m % 2, a, i * P:(i + 1) * P], w3_s[:, c, m, :],
                                       start=(m == 0 and n == 0 and i % 2 == 0),
                                       stop=(m == units - 1 and n == 2), skip_group_check=True)
                mm.then_inc(y_full, 1)

            for m in range(units):
                up(m)
                if m >= 1:
                    down(m - 1)
            if not last:
                work.turn(pe, j + 1)
            down(units - 1)

        def split_x_high(act, j):
            for k in range(KC):
                act.wait_ge(x_turned, j * KC + k + 1)
                if k == 0:
                    wait_if_any(act, h2_full, j * units)
                act.activation(xT[:, HI, k, :], x_ps[k][:], ACT.Copy).then_inc(xT_hi, 1)

        def scalar(act, j, last, between=lambda m: None):
            for m in range(units):
                between(m)
                n = j * units + m
                act.wait_ge(h1_full, n + 1)
                wait_if_any(act, hidden_ready, n - 1)
                act.activation(gate[:, m % 2, :], h1_ps[m % 2][:], ACT.Silu).then_inc(gate_ready, 1)
                act.wait_ge(hidden_ready, n + 1)
                wait_if_any(act, y_full, n - 1)
                act.activation(h_s[:, m % 2, HI, :], hidden[:, m % 2, :], ACT.Copy).then_inc(h_hi, 1)
            if not last:
                work.split_x_high(act, j + 1)
            act.wait_ge(y_full, (j + 1) * units)
            wait_if_any(act, stored, j * 16)
            for n in range(2):
                act.activation(out[:, 2 * n:2 * n + 2, :],
                               y_ps[n][:].rearrange("p (i c) -> p i c", c=C), ACT.Copy).then_inc(out_ready, 1)

        def split_x_low(dve, j):
            for k in range(KC):
                dve.wait_ge(xT_hi, j * KC + k + 1)
                dve.tensor_tensor(xT[:, LO, k, :], x_ps[k][:], xT[:, HI, k, :].bitcast(F32),
                                  ALU.subtract).then_inc(xT_lo, 1)

        def vector(dve, j, last, between=lambda m: None):
            for m in range(units):
                n = j * units + m
                dve.wait_ge(h2_full, n + 1)
                dve.wait_ge(gate_ready, n + 1)
                wait_if_any(dve, h_lo, n - 1)
                dve.tensor_tensor(hidden[:, m % 2, :], h2_ps[m % 2][:], gate[:, m % 2, :],
                                  ALU.mult).then_inc(hidden_ready, 1)
                if m < units - 1:
                    between(m)
                dve.wait_ge(h_hi, n + 1)
                dve.tensor_tensor(h_s[:, m % 2, LO, :], hidden[:, m % 2, :], h_s[:, m % 2, HI, :].bitcast(F32),
                                  ALU.subtract).then_inc(h_lo, 1)
            if not last:
                work.split_x_low(dve, j + 1)
            between(units - 1)

        def all_stored(engine):
            engine.wait_ge(stored, 16 * blocks)

        def wait_stored(engine, j):
            engine.wait_ge(stored, 16 * (j + 1))

    return work


def peeled(engine, count, slot_work, heads=1):
    for j in range(heads):
        slot_work(j, j == 0, False)
    with engine.Fori(heads, count - 1) as j:
        slot_work(j, False, False)
    slot_work(count - 1, False, True)


def split_weights(sem, loads, stage):
    loaded = [sem("weights_loaded0"), sem("weights_loaded1")]
    high, low = sem("weights_high"), sem("weights_low")

    def load(sp, numbers):
        for n in numbers:
            src, split, shape = loads[n]
            wait_if_any(sp, low, n - 1)
            sp.dma_start(shape(stage[:, n % 2, :]), src).then_inc(loaded[n % 2], 16)

    def make_high(act, numbers):
        for n in numbers:
            src, split, shape = loads[n]
            act.wait_ge(loaded[n % 2], 16 * (n // 2 + 1))
            act.activation(split(HI), shape(stage[:, n % 2, :]), ACT.Copy).then_inc(high, 1)

    def make_low(dve, numbers):
        for n in numbers:
            src, split, shape = loads[n]
            dve.wait_ge(high, n + 1)
            dve.tensor_tensor(split(LO), shape(stage[:, n % 2, :]), split(HI).bitcast(F32),
                              ALU.subtract).then_inc(low, 1)

    return load, make_high, make_low, low


def routing_phase(nc, xn2, xs, logits, expert_bias, lanes, masks, shared_w, expert_w, shared_out,
                  w1_s, w2_s, w3_s, w12_s, we3_s, ident, dest, gates, tile_expert):
    half = BLOCKS // 2
    with ExitStack() as ctx:
        def sb(name, shape, dt=F32):
            return ctx.enter_context(nc.sbuf_tensor(name, shape, dt))

        def sem(name):
            return ctx.enter_context(nc.semaphore(name))

        shared = shared_ffn(nc, ctx, "sh0", xn2, shared_out, w1_s, w2_s, w3_s, ident, 0, half)
        stage = sb("stage", [P, 2, 1024])
        x_tiles = sb("x_tiles", [P, 2, NT, C])
        dest_now = sb("dest_now", [P, 2, NT, TOP_K], mybir.dt.int32)
        room = x_tiles[:].rearrange("p a i c -> p (a i c)").rearrange("p (n t e) -> p n t e", n=4, e=NE)
        prob, value, first, second = (room[:, n] for n in range(4))
        best = sb("route_best", [P, TOKEN_TILES])
        chosen = sb("route_chosen", [P, TOKEN_TILES, NE], BF16)
        sums = [sb("route_sums0", [P, 2 * TOKEN_TILES, NE]), sb("route_sums1", [P, 2 * TOKEN_TILES, NE])]
        bias = sb("route_bias", [P, NE])
        lane = sb("route_lane", [P, NE])
        upper = sb("route_upper", [P, P], BF16)
        ones = sb("route_ones", [P, P], BF16)
        mask_f = sb("route_mask", [P, P])
        count_f = sb("route_count", [P, NE])
        count_i = sb("route_count_i", [P, 2, NE], mybir.dt.int32)
        tiles_f = sb("route_tiles", [P, NE])
        ends = [sb("route_ends0", [P, 2 * NE]), sb("route_ends1", [P, 2 * NE])]
        base = sb("route_base", [P, NE])
        picked = sb("route_picked", [P, TOKEN_TILES])
        tile_no = sb("route_tile_no", [1, TILES])
        match = sums[0][:, TOKEN_TILES:, :]
        slot = sums[1][:, 0:TOKEN_TILES, :]
        tile_acc = sums[1][0:1, TOKEN_TILES:, :].rearrange("p t e -> p (t e)")[:, 0:2 * TILES].rearrange(
            "p (n t) -> p n t", n=2)
        rank_ps, total_ps = shared.x_psum

        small_loaded = sem("small_loaded")
        exp_done = sem("exp_done")
        step_done = sem("step_done")
        chosen_ready = sem("chosen_ready")
        rank_ready = sem("rank_ready")
        placed = sem("placed")
        routed = sem("routed")
        rows_loaded = [sem("rows_loaded0"), sem("rows_loaded1")]
        dest_copied = [sem("dest_copied0"), sem("dest_copied1")]
        rows_sent = [sem("rows_sent0"), sem("rows_sent1")]

        x_rows = xn2.rearrange("b (i p) c -> b p i c", p=P)
        load_w, split_high, split_low, w_low = split_weights(sem, [*shared_w, *expert_w], stage)
        halves = 2
        units = HID // P
        expert_numbers = range(len(shared_w), len(shared_w) + len(expert_w))

        def to_split(j, m):
            if isinstance(j, int) and j == 0 and m < len(shared_w) - 2:
                return (m + 2,)
            if isinstance(j, int) and j == 2:
                n = len(expert_w) // units
                return expert_numbers[m * n:(m + 1) * n]
            return ()

        block = ctx.enter_context(nc.Block())

        @block.sync
        def _(sp):
            load_w(sp, range(1))
            shared.load(sp, 0)
            load_w(sp, range(1, 2))
            sp.dma_start(bias[:], expert_bias.partition_broadcast(P)).then_inc(small_loaded, 16)
            sp.dma_start(lane[:], lanes[0:P * NE].rearrange("(p e) -> p e", e=NE)).then_inc(small_loaded, 16)
            sp.dma_start(tile_no[:], lanes[P * NE:P * NE + TILES].rearrange("(p n) -> p n", p=1)).then_inc(small_loaded, 16)
            sp.dma_start(mask_f[:], masks[2]).then_inc(small_loaded, 16)
            load_w(sp, range(2, len(shared_w)))

            def work(j, first_, last):
                if not last:
                    shared.load(sp, j + 1)
                if isinstance(j, int) and j == 1:
                    load_w(sp, expert_numbers[:2])
                if isinstance(j, int) and j == 2:
                    load_w(sp, expert_numbers[2:])
                shared.store(sp, j)

            peeled(sp, half, work, heads=3)
            shared.all_stored(sp)
            for q in range(2):
                sp.wait_ge(rows_sent[q], half * 16 * NT * TOP_K)

        @block.gpsimd
        def _(pool):
            def load_rows(c, q):
                pool.dma_start(x_tiles[:, q], rows_of(x_rows, c)).then_inc(rows_loaded[q], 16)

            def send(c, q, nth):
                tile = c * NT
                now = dest[:, tile:tile + NT, :] if isinstance(c, int) else dest[:, bass.ds(tile, NT), :]
                pool.wait_ge(small_loaded, 64)
                pool.wait_ge(rows_loaded[q], nth * 16)
                pool.tensor_copy(dest_now[:, q], now).then_inc(dest_copied[q], 1)
                pool.wait_ge(small_loaded, 64)
                pool.wait_ge(dest_copied[q], nth)
                for i in range(NT):
                    for k in range(TOP_K):
                        pool.indirect_dma_start(
                            xs[:, :], bass.IndirectOffsetOnAxis(ap=dest_now[:, q, i, k:k + 1], axis=0),
                            x_tiles[:, q, i, :], None).then_inc(rows_sent[q], 16)

            pool.wait_ge(routed, 1)
            for q in range(2):
                load_rows(q, q)
            for q in range(2):
                send(q, q, 1)
            with pool.Fori(2, half + 1) as nth:
                for q in range(2):
                    pool.wait_ge(small_loaded, 64)
                    pool.wait_ge(rows_sent[q], (nth - 1) * 16 * NT * TOP_K)
                    load_rows(2 * nth - 2 + q, q)
                for q in range(2):
                    send(2 * nth - 2 + q, q, nth)

        @block.tensor
        def _(pe):
            def ranks():
                pe.wait_ge(chosen_ready, 1)
                rows = chosen[:].rearrange("p t e -> p (t e)")
                pe.matmul(rank_ps[:], upper[:], rows, start=True, stop=True)
                pe.matmul(total_ps[:], ones[:], rows, start=True, stop=True).then_inc(rank_ready, 1)

            def work(j, first_, last):
                def before_up(m):
                    if first_ and m % (units // halves) == 0:
                        pe.wait_ge(w_low, m // (units // halves) * 3 + 2)

                def before_down(m):
                    if first_ and m % (units // halves) == 0:
                        pe.wait_ge(w_low, m // (units // halves) * 3 + 3)
                    if isinstance(j, int) and j == 1 and m == 1:
                        ranks()
                    if isinstance(j, int) and j == 1 and m == units - 2:
                        pe.wait_ge(placed, 1)

                shared.tensor(pe, j, last, before_up, before_down)

            shared.turn(pe, 0)
            peeled(pe, half, work, heads=3)

        @block.scalar
        def _(act):
            split_high(act, range(2))
            shared.split_x_high(act, 0)
            act.activation(prob, logits[:], ACT.Exp, scale=-1.0).then_inc(exp_done, 1)
            peeled(act, half, lambda j, first_, last: shared.scalar(
                act, j, last, lambda m: split_high(act, to_split(j, m))), heads=3)

        @block.vector
        def _(dve):
            steps = [0]

            def step(instruction):
                steps[0] += 1
                instruction.then_inc(step_done, 1)
                dve.wait_ge(step_done, steps[0])

            by_tile = [P, TOKEN_TILES, NE]

            def over_tiles(a):
                return a.unsqueeze(1).broadcast_to(by_tile)

            def over_experts(a):
                return a.unsqueeze(2).broadcast_to(by_tile)

            def find_best():
                step(dve.tensor_reduce(best[:], value, AX_X, ALU.max))
                step(dve.tensor_tensor(match, value, over_experts(best[:]), ALU.is_equal))

            def take_best(out):
                step(dve.tensor_tensor(match, match, over_tiles(lane[:]), ALU.mult))
                step(dve.tensor_reduce(best[:], match, AX_X, ALU.max))
                step(dve.tensor_tensor(out, match, over_experts(best[:]), ALU.is_equal))

            def set_up():
                dve.wait_ge(small_loaded, 64)
                dve.tensor_copy(upper[:], mask_f[:])
                dve.memset(ones[:], 1.0)
                dve.memset(sums[0][:, 0:TOKEN_TILES, :], 0.0)
                dve.memset(sums[1][:, 0:TOKEN_TILES, :], 0.0)
                dve.memset(ends[0][:, 0:NE], 0.0)
                dve.memset(ends[1][:, 0:NE], 0.0)

            def score():
                dve.wait_ge(exp_done, 1)
                step(dve.tensor_scalar(prob, prob, 1.0, None, ALU.add))
                step(dve.reciprocal(prob, prob))
                step(dve.tensor_tensor(value, prob, over_tiles(bias[:]), ALU.add))

            doublings = TOKEN_TILES.bit_length() - 1
            upto = sums[doublings % 2]
            end = ends[(NE.bit_length() - 1) % 2][:, NE:]

            def add_up(stages):
                for n in stages:
                    src, dst, reach = sums[n % 2], sums[(n + 1) % 2], 1 << n
                    if n == 0:
                        dve.wait_ge(rank_ready, 1)
                        step(dve.tensor_copy(src[:, TOKEN_TILES:, :], total_ps[:].rearrange("p (t e) -> p t e", e=NE)))
                    step(dve.tensor_tensor(dst[:, TOKEN_TILES:, :], src[:, TOKEN_TILES:, :],
                                           src[:, TOKEN_TILES - reach:2 * TOKEN_TILES - reach, :], ALU.add))

            def count():
                step(dve.tensor_scalar(count_i[:, 0, :], upto[:, 2 * TOKEN_TILES - 1, :], float(P - 1), None, ALU.add))
                step(dve.tensor_scalar(count_i[:, 1, :], count_i[:, 0, :], P.bit_length() - 1, None,
                                       ALU.logical_shift_right))
                step(dve.tensor_copy(tiles_f[:], count_i[:, 1, :]))
                step(dve.tensor_copy(ends[0][:, NE:], tiles_f[:]))
                for n in range(NE.bit_length() - 1):
                    src, dst, reach = ends[n % 2], ends[(n + 1) % 2], 1 << n
                    step(dve.tensor_tensor(dst[:, NE:], src[:, NE:], src[:, NE - reach:2 * NE - reach], ALU.add))
                step(dve.tensor_tensor(base[:], end, tiles_f[:], ALU.subtract))
                step(dve.tensor_scalar(base[:], base[:], float(P), None, ALU.mult))

            def place():
                step(dve.tensor_tensor(slot, upto[:, TOKEN_TILES:, :],
                                       total_ps[:].rearrange("p (t e) -> p t e", e=NE), ALU.subtract))
                step(dve.tensor_tensor(slot, slot, rank_ps[:].rearrange("p (t e) -> p t e", e=NE), ALU.add))
                dve.tensor_tensor(slot, slot, over_tiles(base[:]), ALU.add).then_inc(placed, 1)
                dve.wait_ge(placed, 1)

            def choose(k, one_hot):
                step(dve.tensor_tensor(value, one_hot, slot, ALU.mult))
                step(dve.tensor_reduce(picked[:], value, AX_X, ALU.add))
                step(dve.tensor_copy(dest[:, :, k], picked[:]))
                step(dve.tensor_tensor(value, one_hot, prob, ALU.mult))
                reduced = dve.tensor_reduce(gates[:, :, k], value, AX_X, ALU.add)
                if k == 0:
                    step(reduced)
                else:
                    reduced.then_inc(routed, 1)

            def name_tiles():
                step(dve.memset(tile_acc[:, 0, :], 0.0))
                for e in range(NE - 1):
                    step(dve.scalar_tensor_tensor(tile_acc[:, (e + 1) % 2, :], tile_no[:], end[0:1, e:e + 1],
                                                  tile_acc[:, e % 2, :], ALU.is_ge, ALU.add))
                step(dve.tensor_copy(tile_expert[:], tile_acc[:, (NE - 1) % 2, :]))

            def work(j, first_, last):
                def between(m):
                    split_low(dve, to_split(j, m))
                    if first_:
                        if m == 1:
                            set_up()
                        if m == 4:
                            score()
                        if m == 5:
                            find_best()
                        if m == 6:
                            take_best(first)
                        if m == 7:
                            step(dve.scalar_tensor_tensor(value, first, TAKEN, value, ALU.mult, ALU.add))
                            find_best()
                    if isinstance(j, int) and j == 1:
                        if m == 0:
                            take_best(second)
                            dve.tensor_tensor(chosen[:], first, second, ALU.add).then_inc(chosen_ready, 1)
                        if m == 2:
                            add_up(range(0, doublings // 2))
                        if m == 3:
                            add_up(range(doublings // 2, doublings))
                        if m == 4:
                            count()
                        if m == 5:
                            place()
                        if m == 6:
                            choose(0, first)
                        if m == 7:
                            choose(1, second)
                    if isinstance(j, int) and j == 2 and m == 0:
                        name_tiles()

                shared.vector(dve, j, last, between)

            split_low(dve, range(2))
            shared.split_x_low(dve, 0)
            peeled(dve, half, work, heads=3)


def experts_phase(nc, xs, ys, w12_s, we3_s, ident, tile_expert):
    with ExitStack() as ctx:
        def sb(name, shape, dt=F32):
            return ctx.enter_context(nc.sbuf_tensor(name, shape, dt))

        def ps(name, cols):
            return [ctx.enter_context(nc.psum_tensor(f"{name}{n}", [P, T], F32))[:, 0:cols] for n in range(2)]

        def sem(name):
            return ctx.enter_context(nc.semaphore(name))

        RING = 4
        x_t = sb("e_x", [P, RING, C])
        xT = sb("e_xT", [P, 2, 2, KC, P], F32R)
        gate = sb("e_gate", [P, 2, HE])
        hidden = sb("e_hidden", [P, 2, HE])
        hT = sb("e_hT", [P, 2, 2, KH, P], F32R)
        y_t = sb("e_y", [P, RING, C])
        x_ps, h_ps, hT_ps, y_ps = ps("e_x_ps", C), ps("e_h_ps", 2 * HE), ps("e_hT_ps", HE), ps("e_y_ps", C)

        loaded = [sem(f"e_loaded{n}") for n in range(RING)]
        stored = [sem(f"e_stored{n}") for n in range(RING)]
        x_turned, x_hi, x_lo = sem("e_x_turned"), sem("e_x_hi"), sem("e_x_lo")
        h_full, gate_ready, hidden_ready = sem("e_h_full"), sem("e_gate_ready"), sem("e_hidden_ready")
        h_turned, h_hi, h_lo = sem("e_h_turned"), sem("e_h_hi"), sem("e_h_lo")
        y_full, y_ready = sem("e_y_full"), sem("e_y_ready")

        xs_tiles = xs.rearrange("(n p) c -> n p c", p=P)
        ys_tiles = ys.rearrange("(n p) c -> n p c", p=P)

        def tile_of(tiles, n):
            return tiles[n] if isinstance(n, int) else tiles[bass.ds(n, 1)].rearrange("n p c -> (n p) c")

        def exists(n):
            return not isinstance(n, int) or 0 <= n < TILES

        def tiles(engine, step):
            for r in range(RING):
                step(r, r)
            with engine.Fori(1, TILES // RING - 1) as g:
                for r in range(RING):
                    step(g * RING + r, r)
            for r in range(RING + 2):
                step(TILES - RING + r, r % RING)

        block = ctx.enter_context(nc.Block())

        @block.sync
        def _(sp):
            for r in range(RING):
                sp.dma_start(x_t[:, r], tile_of(xs_tiles, r)).then_inc(loaded[r], 16)

            def step(n, r):
                if exists(n + RING):
                    sp.wait_ge(x_turned, n + 1)
                    sp.dma_start(x_t[:, r], tile_of(xs_tiles, n + RING)).then_inc(loaded[r], 16)
                if exists(n - 2):
                    sp.wait_ge(y_ready, n - 1)
                    sp.dma_start(tile_of(ys_tiles, n - 2), y_t[:, (r - 2) % RING]).then_inc(stored[(r - 2) % RING], 16)

            tiles(sp, step)
            for r in range(RING):
                sp.wait_ge(stored[r], TILES // RING * 16)

        @block.tensor
        def _(pe):
            def turn_x(n, r, group):
                pe.wait_ge(loaded[r], group * 16)
                wait_if_any(pe, x_lo, n - 1)
                for k in range(KC):
                    mm = pe.transpose(x_ps[r % 2][:, k * P:(k + 1) * P], x_t[:, r, k * P:(k + 1) * P], ident)
                mm.then_inc(x_turned, 1)

            expert_regs = [pe.alloc_register(f"tile_expert{r}") for r in range(RING)]

            def load_expert(n, r):
                at = tile_expert[0:1, n:n + 1] if isinstance(n, int) else tile_expert[0:1, bass.ds(n, 1)]
                pe.reg_load(expert_regs[r], at)

            def expert_of(r):
                return pe.snap(expert_regs[r], min_val=0, max_val=NE - 1)

            def up(n, r):
                e = expert_of(r)
                pe.wait_ge(x_lo, n + 1)
                wait_if_any(pe, hidden_ready, n - 1)
                m = 0
                for a, c in PASSES:
                    for k in range(KC):
                        mm = pe.matmul(h_ps[r % 2], xT[:, r % 2, a, k, :],
                                       w12_s[:, bass.ds(e, 1), c, k, :].rearrange("p e n -> p (e n)"),
                                       start=(m == 0), stop=(m == 3 * KC - 1))
                        m += 1
                mm.then_inc(h_full, 1)

            def turn_h(n, r):
                pe.wait_ge(hidden_ready, n + 1)
                wait_if_any(pe, h_lo, n - 1)
                for k in range(KH):
                    mm = pe.transpose(hT_ps[r % 2][:, k * P:(k + 1) * P], hidden[:, r % 2, k * P:(k + 1) * P], ident)
                mm.then_inc(h_turned, 1)

            def down(n, r):
                e = expert_of(r)
                pe.wait_ge(h_lo, n + 1)
                wait_if_any(pe, y_ready, n - 1)
                m = 0
                for a, c in PASSES:
                    for k in range(KH):
                        mm = pe.matmul(y_ps[r % 2], hT[:, r % 2, a, k, :],
                                       we3_s[:, bass.ds(e, 1), c, k, :].rearrange("p e n -> p (e n)"),
                                       start=(m == 0), stop=(m == 3 * KH - 1))
                        m += 1
                mm.then_inc(y_full, 1)

            turn_x(0, 0, 1)
            turn_x(1, 1, 1)
            load_expert(0, 0)

            def step(n, r):
                if exists(n + 1):
                    load_expert(n + 1, (r + 1) % RING)
                if exists(n):
                    up(n, r)
                if exists(n - 1):
                    turn_h(n - 1, (r - 1) % RING)
                if exists(n + 2):
                    turn_x(n + 2, (r + 2) % RING, group_of[0] + 1 + (r + 2 >= RING))
                if exists(n - 2):
                    down(n - 2, (r - 2) % RING)

            group_of = [0]
            for r in range(RING):
                step(r, r)
            with pe.Fori(1, TILES // RING - 1) as g:
                group_of[0] = g
                for r in range(RING):
                    step(g * RING + r, r)
            group_of[0] = TILES // RING - 1
            for r in range(RING + 2):
                step(TILES - RING + r, r % RING)

        @block.scalar
        def _(act):
            def x_high(n, r):
                act.wait_ge(x_turned, n + 1)
                wait_if_any(act, h_full, n - 1)
                act.activation(xT[:, r % 2, HI].rearrange("p k t -> p (k t)"), x_ps[r % 2],
                               ACT.Copy).then_inc(x_hi, 1)

            def step(n, r):
                if exists(n):
                    act.wait_ge(h_full, n + 1)
                    wait_if_any(act, hidden_ready, n - 1)
                    act.activation(gate[:, r % 2, :], h_ps[r % 2][:, 0:HE], ACT.Silu).then_inc(gate_ready, 1)
                if exists(n - 1):
                    act.wait_ge(h_turned, n)
                    wait_if_any(act, y_full, n - 2)
                    act.activation(hT[:, (r - 1) % 2, HI].rearrange("p k t -> p (k t)"), hT_ps[(r - 1) % 2],
                                   ACT.Copy).then_inc(h_hi, 1)
                if exists(n + 2):
                    x_high(n + 2, r)
                if exists(n - 2):
                    act.wait_ge(y_full, n - 1)
                    if not isinstance(n, int) or n - 2 >= RING:
                        act.wait_ge(stored[(r - 2) % RING], group_of[0] * 16 - (16 if r < 2 else 0))
                    act.activation(y_t[:, (r - 2) % RING, :], y_ps[r % 2], ACT.Copy).then_inc(y_ready, 1)

            group_of = [0]
            x_high(0, 0)
            x_high(1, 1)
            for r in range(RING):
                step(r, r)
            with act.Fori(1, TILES // RING - 1) as g:
                group_of[0] = g
                for r in range(RING):
                    step(g * RING + r, r)
            for r in range(RING + 2):
                group_of[0] = TILES // RING - 1 + r // RING
                step(TILES - RING + r, r % RING)

        @block.vector
        def _(dve):
            def x_low(n, r):
                dve.wait_ge(x_hi, n + 1)
                dve.tensor_tensor(xT[:, r % 2, LO].rearrange("p k t -> p (k t)"), x_ps[r % 2],
                                  xT[:, r % 2, HI].rearrange("p k t -> p (k t)").bitcast(F32),
                                  ALU.subtract).then_inc(x_lo, 1)

            def step(n, r):
                if exists(n):
                    dve.wait_ge(gate_ready, n + 1)
                    wait_if_any(dve, h_turned, n - 1)
                    dve.tensor_tensor(hidden[:, r % 2, :], h_ps[r % 2][:, HE:2 * HE], gate[:, r % 2, :],
                                      ALU.mult).then_inc(hidden_ready, 1)
                if exists(n - 1):
                    dve.wait_ge(h_hi, n)
                    dve.tensor_tensor(hT[:, (r - 1) % 2, LO].rearrange("p k t -> p (k t)"), hT_ps[(r - 1) % 2],
                                      hT[:, (r - 1) % 2, HI].rearrange("p k t -> p (k t)").bitcast(F32),
                                      ALU.subtract).then_inc(h_lo, 1)
                if exists(n + 2):
                    x_low(n + 2, r)

            x_low(0, 0)
            x_low(1, 1)
            tiles(dve, step)


def combine_phase(nc, xn2, x1, ys, shared_out, w1_s, w2_s, w3_s, ident, dest, gates, out):
    half = BLOCKS // 2
    with ExitStack() as ctx:
        def sb(name, shape, dt=F32):
            return ctx.enter_context(nc.sbuf_tensor(name, shape, dt))

        def sem(name):
            return ctx.enter_context(nc.semaphore(name))

        shared = shared_ffn(nc, ctx, "sh1", xn2, shared_out, w1_s, w2_s, w3_s, ident, half, half)
        from_experts = sb("c_experts", [P, 2, NT, TOP_K, C])
        from_shared = sb("c_shared", [P, 2, NT, C])
        residual = sb("c_residual", [P, 2, NT, C])
        dest_now = sb("c_dest", [P, 2, NT, TOP_K], mybir.dt.int32)
        gate_now = sb("c_gate", [P, 2, NT, TOP_K])
        stats = sb("c_stats", [P, NT, 6])
        mv = sb("c_mv", [P, NT, 2])
        vare = sb("c_vare", [P, NT])
        rstd = sb("c_rstd", [P, NT])
        eps_t = sb("c_eps", [P, NT])
        mhalf_t = sb("c_mhalf", [P, NT])

        gathered = [sem("c_gathered0"), sem("c_gathered1")]
        loaded = [sem("c_loaded0"), sem("c_loaded1")]
        numbers_ready = [sem("c_numbers0"), sem("c_numbers1")]
        summed = sem("c_summed")
        added = sem("c_added")
        gates_ready = sem("c_gates")
        stat_ready = sem("c_stat")
        mv_ready = sem("c_mv_ready")
        vare_ready = sem("c_vare_ready")
        rstd_ready = sem("c_rstd_ready")
        normed = sem("c_normed")
        out_ready = sem("c_out_ready")
        out_stored = [sem("c_stored0"), sem("c_stored1")]
        consts = sem("c_consts")

        def rows(a):
            return a.rearrange("b (i p) c -> b p i c", p=P)

        block = ctx.enter_context(nc.Block())

        def blocks_of(j):
            return ((2 * j + q, q) for q in range(2))

        @block.sync
        def _(sp):
            def load_residual(c, q):
                sp.dma_start(residual[:, q], rows_of(rows(x1), c)).then_inc(loaded[q], 16)

            def load_shared(c, q):
                sp.dma_start(from_shared[:, q], rows_of(rows(shared_out), c)).then_inc(loaded[q], 16)

            def store(c, q, stores):
                sp.wait_ge(out_ready, c + 1)
                sp.dma_start(rows_of(rows(out), c), residual[:, q]).then_inc(out_stored[q], 16)
                sp.wait_ge(out_stored[q], stores * 16)

            def work(j, first_, last):
                if not last:
                    shared.load(sp, j + 1)
                if not first_:
                    store(2 * j - 1, 1, j)
                load_residual(2 * j + 1, 1)
                if not last:
                    load_shared(2 * j + 1, 1)
                store(2 * j, 0, j + 1)
                if not last:
                    load_residual(2 * j + 2, 0)
                if last:
                    store(2 * j + 1, 1, j + 1)
                else:
                    shared.store(sp, j)
                    shared.wait_stored(sp, j)
                    load_shared(2 * j + 2, 0)

            shared.load(sp, 0)
            load_residual(0, 0)
            load_shared(0, 0)
            peeled(sp, half, work)

        @block.gpsimd
        def _(pool):
            def fetch(c, q, nth, first_):
                tile = c * NT
                now = dest[:, tile:tile + NT, :] if isinstance(c, int) else dest[:, bass.ds(tile, NT), :]
                if not first_:
                    pool.wait_ge(consts, 1)
                    pool.wait_ge(summed, c - 1)
                pool.tensor_copy(dest_now[:, q], now).then_inc(numbers_ready[q], 1)
                pool.wait_ge(consts, 1)
                pool.wait_ge(numbers_ready[q], nth)
                for i in range(NT):
                    for k in range(TOP_K):
                        pool.indirect_dma_start(
                            from_experts[:, q, i, k, :], None, ys[:, :],
                            bass.IndirectOffsetOnAxis(ap=dest_now[:, q, i, k:k + 1], axis=0)).then_inc(gathered[q], 16)

            def invert(c):
                pool.wait_ge(mv_ready, c + 1)
                pool.tensor_tensor(vare[:], mv[:, :, 1], eps_t[:], ALU.add).then_inc(vare_ready, 1)
                pool.wait_ge(vare_ready, c + 1)
                pool.tensor_tensor(rstd[:], vare[:], mhalf_t[:], ALU.pow).then_inc(rstd_ready, 1)

            def add(c, q):
                pool.wait_ge(normed, c + 1)
                pool.tensor_tensor(residual[:, q], residual[:, q], from_shared[:, q], ALU.add).then_inc(out_ready, 1)

            pool.memset(eps_t[:], EPS)
            pool.memset(mhalf_t[:], -0.5).then_inc(consts, 1)
            pool.wait_ge(consts, 1)
            for q in range(2):
                fetch(q, q, 1, True)
            with pool.Fori(2, half + 1) as nth:
                for c, q in blocks_of(nth - 2):
                    invert(c)
                    fetch(c + 2, q, nth, False)
                    add(c, q)
            invert(2 * half - 2)
            add(2 * half - 2, 0)
            invert(2 * half - 1)

        @block.tensor
        def _(pe):
            shared.turn(pe, 0)
            peeled(pe, half, lambda j, first_, last: shared.tensor(pe, j, last))

        @block.scalar
        def _(act):
            shared.split_x_high(act, 0)
            peeled(act, half, lambda j, first_, last: shared.scalar(act, j, last))

        @block.vector
        def _(dve):
            def add_expert(c, q, j, k):
                if k == 0:
                    tile = c * NT
                    now = gates[:, tile:tile + NT, :] if isinstance(c, int) else gates[:, bass.ds(tile, NT), :]
                    dve.tensor_copy(gate_now[:, q], now).then_inc(gates_ready, 1)
                    dve.wait_ge(gates_ready, c + 1)
                    dve.wait_ge(loaded[q], (j + 1) * 32)
                    dve.wait_ge(gathered[q], (j + 1) * 16 * NT * TOP_K)
                else:
                    dve.wait_ge(added, c + 1)
                for i in range(NT):
                    ad = dve.scalar_tensor_tensor(from_shared[:, q, i, :], from_experts[:, q, i, k, :],
                                                  gate_now[:, q, i, k:k + 1], from_shared[:, q, i, :],
                                                  ALU.mult, ALU.add)
                ad.then_inc(summed if k else added, 1)

            def moments(c, q):
                dve.wait_ge(summed, c + 1)
                for i in range(NT):
                    st = dve.bn_stats(stats[:, i, :], from_shared[:, q, i, :])
                st.then_inc(stat_ready, 1)
                dve.wait_ge(gates_ready, 1)
                dve.wait_ge(stat_ready, c + 1)
                for i in range(NT):
                    ag = dve.bn_aggr(mv[:, i, :], stats[:, i, :])
                ag.then_inc(mv_ready, 1)

            def normalize(c, q):
                dve.wait_ge(rstd_ready, c + 1)
                for i in range(NT):
                    nm = dve.tensor_scalar(from_shared[:, q, i, :], from_shared[:, q, i, :], mv[:, i, 0:1],
                                           rstd[:, i:i + 1], ALU.subtract, ALU.mult)
                nm.then_inc(normed, 1)

            def sum_experts_last(c, q, j):
                dve.tensor_copy(gate_now[:, q], gates[:, c * NT:(c + 1) * NT, :]).then_inc(gates_ready, 1)
                dve.wait_ge(gates_ready, c + 1)
                dve.wait_ge(gathered[q], (j + 1) * 16 * NT * TOP_K)
                dve.wait_ge(out_ready, c - 1)
                for i in range(NT):
                    ad = dve.tensor_scalar(from_shared[:, q, i, :], from_experts[:, q, i, 0, :],
                                           gate_now[:, q, i, 0:1], None, ALU.mult)
                ad.then_inc(added, 1)
                dve.wait_ge(added, c + 1)
                for i in range(NT):
                    ad = dve.scalar_tensor_tensor(from_shared[:, q, i, :], from_experts[:, q, i, 1, :],
                                                  gate_now[:, q, i, 1:2], from_shared[:, q, i, :],
                                                  ALU.mult, ALU.add)
                ad.then_inc(added, 1)

            def finish_last(c, q, j):
                dve.wait_ge(added, c + 2)
                dve.wait_ge(shared.output_ready, (j + 1) * 2)
                dve.tensor_tensor(from_shared[:, q], from_shared[:, q], shared.output[:], ALU.add).then_inc(summed, 1)
                moments(c, q)
                normalize(c, q)
                dve.wait_ge(normed, c + 1)
                dve.wait_ge(loaded[q], (j + 1) * 32 - 16)
                dve.tensor_tensor(residual[:, q], residual[:, q], from_shared[:, q], ALU.add).then_inc(out_ready, 1)

            def work(j, first_, last):
                def between(m):
                    if m == 0 and not first_:
                        normalize(2 * j - 1, 1)
                    if m in (1, 2):
                        add_expert(2 * j, 0, j, m - 1)
                    if m == 3:
                        moments(2 * j, 0)
                    if m == 4:
                        normalize(2 * j, 0)
                    if m in (5, 6) and not last:
                        add_expert(2 * j + 1, 1, j, m - 5)
                    if m == 7 and not last:
                        moments(2 * j + 1, 1)
                    if m == 5 and last:
                        sum_experts_last(2 * j + 1, 1, j)

                shared.vector(dve, j, last, between)
                if last:
                    finish_last(2 * j + 1, 1, j)

            shared.split_x_low(dve, 0)
            peeled(dve, half, work)


def model(nc, x, wq, wk, wv, wo, w12T, w3T, sw1T, sw2T, sw3T, router_wT, expert_bias, rope_tables, masks, lanes, out):
    def dram(name, shape):
        return nc.dram_tensor(name, shape, F32, kind="Internal").ap()

    x1, xn2, shared_out = dram("x1", (B, T, C)), dram("xn2", (B, T, C)), dram("shared_out", (B, T, C))
    xs, ys = dram("expert_rows", (TILES * P, C)), dram("expert_results", (TILES * P, C))

    with ExitStack() as ctx:
        logits = ctx.enter_context(nc.sbuf_tensor("logits", [P, TOKEN_TILES, NE], F32))
        attention_phase(nc, x, wq, wk, wv, wo, router_wT, rope_tables, masks, x1, xn2, xs, logits)

        def sb(name, shape, dt=F32):
            return ctx.enter_context(nc.sbuf_tensor(name, shape, dt))

        w1_s, w2_s = (sb(n, [P, 2, KC, HID], F32R) for n in ("shared_w1_split", "shared_w2_split"))
        w3_s = sb("shared_w3_split", [P, 2, HID // P, C], F32R)
        ident = sb("ident", [P, P])
        dest = sb("dest", [P, TOKEN_TILES, TOP_K], mybir.dt.int32)
        gates = sb("gates", [P, TOKEN_TILES, TOP_K])
        experts = ctx.enter_context(ExitStack())
        w12_s = experts.enter_context(nc.sbuf_tensor("w12_split", [P, NE, 2, KC, 2 * HE], F32R))
        we3_s = experts.enter_context(nc.sbuf_tensor("w3_split", [P, NE, 2, KH, C], F32R))
        tile_expert = experts.enter_context(nc.sbuf_tensor("tile_expert", [1, TILES], mybir.dt.int32))

        with nc.semaphore("ident_loaded") as ident_loaded, nc.Block() as block:
            @block.sync
            def _(sp):
                sp.dma_start(ident[:], masks[0]).then_inc(ident_loaded, 16)
                sp.wait_ge(ident_loaded, 16)

        def by_rows(src, split, cols):
            return src.rearrange("(k p) n -> p k n", p=P), split, lambda a: a.rearrange("p (k n) -> p k n", n=cols)

        shared_w = []
        for n in range(0, HID, 512):
            for w, split in ((sw1T, w1_s), (sw2T, w2_s)):
                shared_w.append(by_rows(w[:, n:n + 512], lambda h, s=split, n=n: s[:, h, :, n:n + 512], 512))
            m = n // P
            shared_w.append(by_rows(sw3T[m * P:(m + 4) * P, :], lambda h, m=m: w3_s[:, h, m:m + 4, :], C))
        expert_w = []
        for e in range(NE):
            expert_w.append(by_rows(w12T[e], lambda h, e=e: w12_s[:, e, h], 2 * HE))
        for e in range(0, NE):
            src, split, shape = by_rows(w3T[e], lambda h, e=e: we3_s[:, e, h], C)
            expert_w.append((src, split, lambda a: a[:, 0:KH * C].rearrange("p (k n) -> p k n", n=C)))

        routing_phase(nc, xn2, xs, logits, expert_bias, lanes, masks, shared_w, expert_w, shared_out,
                      w1_s, w2_s, w3_s, w12_s, we3_s, ident[:], dest, gates, tile_expert)
        experts_phase(nc, xs, ys, w12_s, we3_s, ident[:], tile_expert)
        experts.close()
        combine_phase(nc, xn2, x1, ys, shared_out, w1_s, w2_s, w3_s, ident[:], dest, gates, out)


def rope_constants():
    inv_freq = np.float32(1) / np.float32(THETA) ** (np.arange(0, D, 2, dtype=np.float32) / np.float32(D))
    angle = (inv_freq[:, None] * np.arange(T, dtype=np.float32)[None, :]).astype(np.float64)
    cos = np.concatenate([np.cos(angle)] * 2)
    sin = np.concatenate([-np.sin(angle), np.sin(angle)])
    scale = 1 / np.sqrt(D)
    return np.stack([cos, sin, cos * scale, sin * scale]).astype(np.float32)


def mask_constants():
    row, col = np.indices((P, P))
    return np.stack([row == col, np.where(col > row, MASKED, 0), col > row]).astype(np.float32)


def lane_constants():
    return np.concatenate([np.tile(NE - np.arange(NE), P), np.arange(TILES)]).astype(np.float32)


_INS = ['L0_attn_hidden_states', 'L0_attn_Wq', 'L0_attn_Wk', 'L0_attn_Wv', 'L0_attn_Wo']
_TURNED = ['L0_ffn_w12', 'L0_ffn_w3', 'L0_ffn_shared_w1', 'L0_ffn_shared_w2', 'L0_ffn_shared_w3', 'L0_ffn_router_w']


def kernel(**inputs):
    import numpy as _np
    import concourse.bacc as _bacc
    from concourse import mybir as _mybir
    from concourse.bass_utils import run_bass_kernel_spmd as _run

    nc = _bacc.Bacc("TRN2", target_bir_lowering=False, num_devices=1)
    arrays, args = {}, []

    def given(name, a):
        arrays[f"in_{name}_dram"] = a
        args.append(nc.dram_tensor(f"in_{name}_dram", a.shape, _mybir.dt.from_np(a.dtype), kind="ExternalInput").ap())

    for name in _INS:
        given(name, _np.ascontiguousarray(inputs[name]))
    for name in _TURNED:
        given(name, _np.ascontiguousarray(_np.swapaxes(inputs[name], -1, -2)))
    given("L0_ffn_expert_bias", _np.ascontiguousarray(inputs["L0_ffn_expert_bias"]))
    given("rope_tables", rope_constants())
    given("masks", mask_constants())
    given("lanes", lane_constants())
    args.append(nc.dram_tensor("out_0_dram", (B, T, C), _mybir.dt.float32, kind="ExternalOutput").ap())
    model(nc, *args)
    r = _run(nc, [arrays], core_ids=[0])
    return r.results[0]["out_0_dram"]
```
